# Optimizing a Trainium2 kernel written in Bass

```python
import numpy as np
import jax
import jax.numpy as jnp

def _softmax(x, axis=-1):
    return jax.nn.softmax(x, axis=axis)
def _gelu(x):
    return jax.nn.gelu(x, approximate=True)
def _silu(x):
    return jax.nn.silu(x)
def _sigmoid(x):
    return jax.nn.sigmoid(x)
def _layernorm(x, axis=-1, eps=1e-5):
    m = jnp.mean(x, axis=axis, keepdims=True)
    v = jnp.var(x, axis=axis, keepdims=True)
    return (x - m) / jnp.sqrt(v + eps)
def _scatter_add(tgt, idx, src, axis=0):
    return tgt.at[idx].add(src)
def _segment_sum(src, seg, n):
    return jax.ops.segment_sum(src, seg, n)

kernel_name = 'mk_conv_preact_d4_conv_nhwc96_04ac01'

def setup_inputs(seed: int = 0):
    np.random.seed(seed)
    _w = jnp.asarray
    def _rec_inputs():
        import jax
        import jax.numpy as jnp
        _gk = jax.random.key(seed)
        x = -0.0005963 + 1.001 * jax.random.normal(jax.random.fold_in(_gk, 1), (8, 64, 64, 96), jnp.float32)
        return x
    x = _rec_inputs()
    def _L0_conv_setup():
        import jax, jax.numpy as jnp
        import numpy as np
        B, H, W = (8, 64, 64)
        D_MODEL, D_STATE, D_INNER, DT_RANK, K = (96, 16, 192, 6, 4)
        EPS = 1e-06

        def _ss2d(x, in_proj_w, conv_w, conv_b, x_proj_w, dt_projs_w, A_logs, Ds, dt_projs_bias, norm_w, norm_b, out_proj_w):
            silu = jax.nn.silu
            Bb, Hh, Ww, _ = x.shape
            L = Hh * Ww
            xz = x @ in_proj_w.T
            xx, z = jnp.split(xz, 2, axis=-1)
            z = silu(z)
            xc = jnp.transpose(xx, (0, 3, 1, 2))
            xc = jax.lax.conv_general_dilated(xc, conv_w, (1, 1), ((1, 1), (1, 1)), dimension_numbers=('NCHW', 'OIHW', 'NCHW'), feature_group_count=D_INNER) + conv_b[None, :, None, None]
            xc = silu(xc)
            x_hw = xc.reshape(Bb, D_INNER, L)
            x_wh = jnp.transpose(xc, (0, 1, 3, 2)).reshape(Bb, D_INNER, L)
            xs = jnp.stack([x_hw, x_wh, x_hw[..., ::-1], x_wh[..., ::-1]], axis=1)
            xpw = x_proj_w.reshape(K, DT_RANK + 2 * D_STATE, D_INNER)
            x_dbl = jnp.einsum('bkdl,kcd->bkcl', xs, xpw)
            dts, Bs, Cs = jnp.split(x_dbl, [DT_RANK, DT_RANK + D_STATE], axis=2)
            dtw = dt_projs_w.reshape(K, D_INNER, DT_RANK)
            dts = jnp.einsum('bkrl,kdr->bkdl', dts, dtw)
            A = -jnp.exp(A_logs).reshape(K, D_INNER, D_STATE)
            dt = jax.nn.softplus(dts + dt_projs_bias.reshape(1, K, D_INNER, 1))

            def step(h, inp):
                u_t, dt_t, B_t, C_t = inp
                dA = jnp.exp(dt_t[..., None] * A)
                h = h * dA + (dt_t * u_t)[..., None] * B_t[:, :, None, :]
                y = jnp.einsum('bkdn,bkn->bkd', h, C_t)
                return (h, y)
            h0 = jnp.zeros((Bb, K, D_INNER, D_STATE), jnp.float32)
            seq = (jnp.moveaxis(xs, -1, 0), jnp.moveaxis(dt, -1, 0), jnp.moveaxis(Bs, -1, 0), jnp.moveaxis(Cs, -1, 0))
            _, ysL = jax.lax.scan(step, h0, seq)
            ys = jnp.moveaxis(ysL, 0, -1)
            ys = ys + xs * Ds.reshape(1, K, D_INNER, 1)
            y = ys[:, 0] + ys[:, 2][..., ::-1]
            yw = ys[:, 1] + ys[:, 3][..., ::-1]
            y = y + yw.reshape(Bb, D_INNER, Ww, Hh).transpose(0, 1, 3, 2).reshape(Bb, D_INNER, L)
            y = y.reshape(Bb, D_INNER, Hh, Ww).transpose(0, 2, 3, 1)
            mean = y.mean(-1, keepdims=True)
            var = ((y - mean) ** 2).mean(-1, keepdims=True)
            y = (y - mean) / jnp.sqrt(var + EPS) * norm_w + norm_b
            y = y * z
            return y @ out_proj_w.T
        key = jax.random.key(seed)
        ks = jax.random.split(key, 9)
        f = lambda k, s, sc=0.02: jax.random.normal(k, s, dtype=jnp.float32) * sc
        return {'x': jax.random.normal(ks[0], (B, H, W, D_MODEL), jnp.float32), 'in_proj_w': f(ks[1], (2 * D_INNER, D_MODEL)), 'conv_w': f(ks[2], (D_INNER, 1, 3, 3), 0.1), 'conv_b': jnp.zeros((D_INNER,), jnp.float32), 'x_proj_w': f(ks[3], (K * (DT_RANK + 2 * D_STATE), D_INNER)), 'dt_projs_w': f(ks[4], (K * D_INNER, DT_RANK), 0.1), 'A_logs': jnp.log(jax.random.uniform(ks[5], (K * D_INNER, D_STATE), jnp.float32, 1.0, 16.0)), 'Ds': jnp.ones((K * D_INNER,), jnp.float32), 'dt_projs_bias': f(ks[6], (K * D_INNER,), 0.5), 'norm_w': jnp.ones((D_INNER,), jnp.float32), 'norm_b': jnp.zeros((D_INNER,), jnp.float32), 'out_proj_w': f(ks[7], (D_MODEL, D_INNER))}
    _L0_conv_all = _L0_conv_setup()
    _L0_conv_in = {k: v for k, v in _L0_conv_all.items() if k in ('in_proj_w', 'conv_w', 'conv_b', 'x_proj_w', 'dt_projs_w', 'A_logs', 'Ds', 'dt_projs_bias', 'norm_w', 'norm_b', 'out_proj_w', )}
    del _L0_conv_all

    def _L1_conv_setup():
        import math
        import jax, jax.numpy as jnp
        import numpy as np
        B_, H_, W_, D_MODEL = (4, 64, 64, 96)
        D_STATE, D_CONV, EXPAND, K_ = (16, 3, 2, 4)
        D_INNER = EXPAND * D_MODEL
        DT_RANK = math.ceil(D_MODEL / 16)

        def _scan_indices(H, W):
            L = H * W
            o1 = []
            for s in range(H + W - 1):
                coords = [i * W + (s - i) for i in range(max(0, s - W + 1), min(H, s + 1))]
                if s % 2 == 1:
                    coords = coords[::-1]
                o1.extend(coords)
            o2 = []
            for s in range(H + W - 1):
                coords = []
                for i in range(max(0, s - W + 1), min(H, s + 1)):
                    j = W - 1 - (s - i)
                    if 0 <= j < W:
                        coords.append(i * W + j)
                if s % 2 == 1:
                    coords = coords[::-1]
                o2.extend(coords)
            cy, cx = (H // 2, W // 2)
            yy, xx = np.meshgrid(np.arange(H), np.arange(W), indexing='ij')
            dy, dx = (yy - cy, xx - cx)
            r = np.sqrt(dy ** 2 + dx ** 2)
            th = np.arctan2(dy, dx)
            o3 = np.argsort((r * (L + 1) + (th + np.pi) * 10).flatten())
            o4 = np.argsort((-r * (L + 1) + (th + np.pi) * 10).flatten())
            idx = np.stack([np.array(o1), np.array(o2), o3, o4]).astype(np.int32)
            inv = np.argsort(idx, axis=1).astype(np.int32)
            return (idx, inv)
        key = jax.random.key(seed)
        ks = jax.random.split(key, 12)
        f = jnp.float32
        x = jax.random.normal(ks[0], (B_, H_, W_, D_MODEL), f)
        in_proj_w = jax.random.normal(ks[1], (2 * D_INNER, D_MODEL), f) * 0.02
        conv_w = jax.random.normal(ks[2], (D_INNER, 1, D_CONV, D_CONV), f) * 0.1
        conv_b = jnp.zeros((D_INNER,), f)
        x_proj_weight = jax.random.normal(ks[3], (K_, DT_RANK + 2 * D_STATE, D_INNER), f) * 0.02
        s = DT_RANK ** (-0.5)
        dt_projs_weight = jax.random.uniform(ks[4], (K_, D_INNER, DT_RANK), f, -s, s)
        dt = jnp.exp(jax.random.uniform(ks[5], (K_, D_INNER), f) * (math.log(0.1) - math.log(0.001)) + math.log(0.001))
        dt = jnp.clip(dt, 0.0001, None)
        dt_projs_bias = dt + jnp.log(-jnp.expm1(-dt))
        A_logs = jnp.log(jnp.tile(jnp.arange(1, D_STATE + 1, dtype=f)[None, :], (K_ * D_INNER, 1)))
        Ds = jnp.ones((K_ * D_INNER,), f)
        direction_Bs = jax.random.normal(ks[6], (K_, D_STATE), f) * 0.02
        pf_w1 = jax.random.normal(ks[7], (32, 2), f) * 0.5
        pf_b1 = jnp.zeros((32,), f)
        pf_w2 = jax.random.normal(ks[8], (K_, 32), f) * 0.1
        pf_b2 = jnp.zeros((K_,), f)
        ln_g = jnp.ones((D_INNER,), f)
        ln_b = jnp.zeros((D_INNER,), f)
        out_proj_w = jax.random.normal(ks[9], (D_MODEL, D_INNER), f) * 0.02
        return dict(x=x, in_proj_w=in_proj_w, conv_w=conv_w, conv_b=conv_b, x_proj_weight=x_proj_weight, dt_projs_weight=dt_projs_weight, dt_projs_bias=dt_projs_bias, A_logs=A_logs, Ds=Ds, direction_Bs=direction_Bs, pf_w1=pf_w1, pf_b1=pf_b1, pf_w2=pf_w2, pf_b2=pf_b2, ln_g=ln_g, ln_b=ln_b, out_proj_w=out_proj_w)
    _L1_conv_all = _L1_conv_setup()
    _L1_conv_in = {k: v for k, v in _L1_conv_all.items() if k in ('in_proj_w', 'conv_w', 'conv_b', 'x_proj_weight', 'dt_projs_weight', 'dt_projs_bias', 'A_logs', 'Ds', 'direction_Bs', 'pf_w1', 'pf_b1', 'pf_w2', 'pf_b2', 'ln_g', 'ln_b', 'out_proj_w', )}
    del _L1_conv_all

    def _L2_conv_setup():
        import math
        import jax, jax.numpy as jnp
        import numpy as np
        D_MODEL = 96
        D_STATE = 16
        D_CONV = 3
        EXPAND = 2
        D_INNER = EXPAND * D_MODEL
        DT_RANK = math.ceil(D_MODEL / 16)
        K = 4
        BATCH = 2
        HH = 64
        WW = 64

        def _selective_scan(u, delta, A, Bm, Cm, D, delta_bias):
            delta = jax.nn.softplus(delta + delta_bias[None, :, :, None])
            dL = jnp.moveaxis(delta, -1, 0)
            uL = jnp.moveaxis(u, -1, 0)
            BL = jnp.moveaxis(Bm, -1, 0)
            CL = jnp.moveaxis(Cm, -1, 0)
            Bsz, Kk, Dn, L = u.shape
            N = A.shape[-1]
            x0 = jnp.zeros((Bsz, Kk, Dn, N), dtype=u.dtype)

            def step(xstate, inp):
                d_l, u_l, b_l, c_l = inp
                dA = jnp.exp(d_l[..., None] * A)
                dBu = d_l[..., None] * b_l[:, None] * u_l[..., None]
                xstate = dA * xstate + dBu
                y = jnp.einsum('bkdn,bdn->bkd', xstate, c_l)
                return (xstate, y)
            _, ys = jax.lax.scan(step, x0, (dL, uL, BL, CL))
            y = jnp.moveaxis(ys, 0, -1)
            return y + u * D[None, :, :, None]
        key = jax.random.key(seed)
        ks = jax.random.split(key, 8)
        x = jax.random.normal(ks[0], (BATCH, HH, WW, D_MODEL), dtype=jnp.float32)
        in_proj_w = jax.random.normal(ks[1], (2 * D_INNER, D_MODEL), jnp.float32) * D_MODEL ** (-0.5)
        conv_w = jax.random.normal(ks[2], (D_INNER, 1, D_CONV, D_CONV), jnp.float32) * (1.0 / 3.0)
        conv_b = jnp.zeros((D_INNER,), jnp.float32)
        x_proj_weight = jax.random.normal(ks[3], (K, DT_RANK + 2 * D_STATE, D_INNER), jnp.float32) * D_INNER ** (-0.5)
        std = DT_RANK ** (-0.5)
        dt_projs_weight = jax.random.uniform(ks[4], (K, D_INNER, DT_RANK), jnp.float32, -std, std)
        dt = jnp.exp(jax.random.uniform(ks[5], (K, D_INNER), jnp.float32) * (math.log(0.1) - math.log(0.001)) + math.log(0.001))
        dt = jnp.clip(dt, 0.0001, None)
        dt_projs_bias = dt + jnp.log(-jnp.expm1(-dt))
        A_logs = jnp.tile(jnp.log(jnp.arange(1, D_STATE + 1, dtype=jnp.float32)), (K * D_INNER, 1))
        Ds = jnp.ones((K * D_INNER,), jnp.float32)
        ln_gamma = jnp.ones((D_INNER,), jnp.float32)
        ln_beta = jnp.zeros((D_INNER,), jnp.float32)
        out_proj_w = jax.random.normal(ks[6], (D_MODEL, D_INNER), jnp.float32) * D_INNER ** (-0.5)
        return dict(x=x, in_proj_w=in_proj_w, conv_w=conv_w, conv_b=conv_b, x_proj_weight=x_proj_weight, dt_projs_weight=dt_projs_weight, dt_projs_bias=dt_projs_bias, A_logs=A_logs, Ds=Ds, ln_gamma=ln_gamma, ln_beta=ln_beta, out_proj_w=out_proj_w)
    _L2_conv_all = _L2_conv_setup()
    _L2_conv_in = {k: v for k, v in _L2_conv_all.items() if k in ('in_proj_w', 'conv_w', 'conv_b', 'x_proj_weight', 'dt_projs_weight', 'dt_projs_bias', 'A_logs', 'Ds', 'ln_gamma', 'ln_beta', 'out_proj_w', )}
    del _L2_conv_all

    def _L3_conv_setup():
        import jax, jax.numpy as jnp
        import numpy as np
        import math
        B_, H_, W_, DM, DE, K_, N_, R_ = (2, 48, 48, 96, 192, 4, 16, 6)

        def _ss2d(x, in_proj_w, conv_w, conv_b, x_proj_weight, dt_projs_weight, dt_projs_bias, A_logs, Ds, ln_gamma, ln_beta, out_proj_w):
            B, H, W, _ = x.shape
            DE = conv_w.shape[0]
            K = x_proj_weight.shape[0]
            N = A_logs.shape[1]
            R = dt_projs_weight.shape[2]
            L = H * W
            xz = jnp.einsum('bhwc,dc->bhwd', x, in_proj_w)
            xh, z = jnp.split(xz, 2, axis=-1)
            z = jax.nn.silu(z)
            xc = jnp.transpose(xh, (0, 3, 1, 2))
            xc = jax.lax.conv_general_dilated(xc, conv_w, (1, 1), 'SAME', dimension_numbers=('NCHW', 'OIHW', 'NCHW'), feature_group_count=DE)
            xc = jax.nn.silu(xc + conv_b[None, :, None, None])
            x_hs = xc.reshape(B, DE, L)
            x_vs = jnp.swapaxes(xc, 2, 3).reshape(B, DE, L)
            xs = jnp.stack([x_hs, x_hs[..., ::-1], x_vs, x_vs[..., ::-1]], axis=1)
            x_dbl = jnp.einsum('bkdl,kcd->bkcl', xs, x_proj_weight)
            dts = x_dbl[:, :, :R]
            Bs = x_dbl[:, :, R:R + N]
            Cs = x_dbl[:, :, R + N:]
            dts = jnp.einsum('bkrl,kdr->bkdl', dts, dt_projs_weight)
            delta = jax.nn.softplus(dts + dt_projs_bias[None, :, :, None])
            A = -jnp.exp(A_logs).reshape(K, DE, N)
            dA = jnp.exp(delta[..., None] * A[None, :, :, None, :])
            dBu = (delta * xs)[..., None] * jnp.swapaxes(Bs, 2, 3)[:, :, None]

            def comb(e1, e2):
                a1, b1 = e1
                a2, b2 = e2
                return (a2 * a1, a2 * b1 + b2)
            _, hstate = jax.lax.associative_scan(comb, (dA, dBu), axis=3)
            ys = jnp.einsum('bkdln,bknl->bkdl', hstate, Cs) + Ds.reshape(K, DE)[None, :, :, None] * xs

            def rev_v(y):
                return jnp.swapaxes(y.reshape(B, DE, W, H), 2, 3).reshape(B, DE, L)
            y = ys[:, 0] + ys[:, 1, :, ::-1] + rev_v(ys[:, 2]) + rev_v(ys[:, 3, :, ::-1])
            y = jnp.swapaxes(y, 1, 2)
            mu = jnp.mean(y, axis=-1, keepdims=True)
            var = jnp.mean(jnp.square(y - mu), axis=-1, keepdims=True)
            y = (y - mu) * jax.lax.rsqrt(var + 1e-05) * ln_gamma + ln_beta
            y = y.reshape(B, H, W, DE).astype(x.dtype)
            return jnp.einsum('bhwd,cd->bhwc', y * z, out_proj_w)
        key = jax.random.key(seed)
        ks = jax.random.split(key, 8)
        x = jax.random.normal(ks[0], (B_, H_, W_, DM), jnp.float32)
        in_proj_w = jax.random.normal(ks[1], (2 * DE, DM), jnp.float32) * DM ** (-0.5)
        conv_w = jax.random.normal(ks[2], (DE, 1, 3, 3), jnp.float32) * (1.0 / 3.0)
        conv_b = jnp.zeros((DE,), jnp.float32)
        x_proj_weight = jax.random.normal(ks[3], (K_, R_ + 2 * N_, DE), jnp.float32) * DE ** (-0.5)
        dt_projs_weight = jax.random.normal(ks[4], (K_, DE, R_), jnp.float32) * R_ ** (-0.5)
        dt = jnp.exp(jax.random.uniform(ks[5], (K_, DE)) * (math.log(0.1) - math.log(0.001)) + math.log(0.001))
        dt_projs_bias = (dt + jnp.log(-jnp.expm1(-dt))).astype(jnp.float32)
        A_logs = jnp.log(jnp.tile(jnp.arange(1, N_ + 1, dtype=jnp.float32), (K_ * DE, 1)))
        Ds = jnp.ones((K_ * DE,), jnp.float32)
        ln_gamma = jnp.ones((DE,), jnp.float32)
        ln_beta = jnp.zeros((DE,), jnp.float32)
        out_proj_w = jax.random.normal(ks[6], (DM, DE), jnp.float32) * DE ** (-0.5)
        return dict(x=x, in_proj_w=in_proj_w, conv_w=conv_w, conv_b=conv_b, x_proj_weight=x_proj_weight, dt_projs_weight=dt_projs_weight, dt_projs_bias=dt_projs_bias, A_logs=A_logs, Ds=Ds, ln_gamma=ln_gamma, ln_beta=ln_beta, out_proj_w=out_proj_w)
    _L3_conv_all = _L3_conv_setup()
    _L3_conv_in = {k: v for k, v in _L3_conv_all.items() if k in ('in_proj_w', 'conv_w', 'conv_b', 'x_proj_weight', 'dt_projs_weight', 'dt_projs_bias', 'A_logs', 'Ds', 'ln_gamma', 'ln_beta', 'out_proj_w', )}
    del _L3_conv_all

    return {
        "x": x,
        "L0_conv_in_proj_w": _L0_conv_in["in_proj_w"],
        "L0_conv_conv_w": _L0_conv_in["conv_w"],
        "L0_conv_conv_b": _L0_conv_in["conv_b"],
        "L0_conv_x_proj_w": _L0_conv_in["x_proj_w"],
        "L0_conv_dt_projs_w": _L0_conv_in["dt_projs_w"],
        "L0_conv_A_logs": _L0_conv_in["A_logs"],
        "L0_conv_Ds": _L0_conv_in["Ds"],
        "L0_conv_dt_projs_bias": _L0_conv_in["dt_projs_bias"],
        "L0_conv_norm_w": _L0_conv_in["norm_w"],
        "L0_conv_norm_b": _L0_conv_in["norm_b"],
        "L0_conv_out_proj_w": _L0_conv_in["out_proj_w"],
        "L1_conv_in_proj_w": _L1_conv_in["in_proj_w"],
        "L1_conv_conv_w": _L1_conv_in["conv_w"],
        "L1_conv_conv_b": _L1_conv_in["conv_b"],
        "L1_conv_x_proj_weight": _L1_conv_in["x_proj_weight"],
        "L1_conv_dt_projs_weight": _L1_conv_in["dt_projs_weight"],
        "L1_conv_dt_projs_bias": _L1_conv_in["dt_projs_bias"],
        "L1_conv_A_logs": _L1_conv_in["A_logs"],
        "L1_conv_Ds": _L1_conv_in["Ds"],
        "L1_conv_direction_Bs": _L1_conv_in["direction_Bs"],
        "L1_conv_pf_w1": _L1_conv_in["pf_w1"],
        "L1_conv_pf_b1": _L1_conv_in["pf_b1"],
        "L1_conv_pf_w2": _L1_conv_in["pf_w2"],
        "L1_conv_pf_b2": _L1_conv_in["pf_b2"],
        "L1_conv_ln_g": _L1_conv_in["ln_g"],
        "L1_conv_ln_b": _L1_conv_in["ln_b"],
        "L1_conv_out_proj_w": _L1_conv_in["out_proj_w"],
        "L2_conv_in_proj_w": _L2_conv_in["in_proj_w"],
        "L2_conv_conv_w": _L2_conv_in["conv_w"],
        "L2_conv_conv_b": _L2_conv_in["conv_b"],
        "L2_conv_x_proj_weight": _L2_conv_in["x_proj_weight"],
        "L2_conv_dt_projs_weight": _L2_conv_in["dt_projs_weight"],
        "L2_conv_dt_projs_bias": _L2_conv_in["dt_projs_bias"],
        "L2_conv_A_logs": _L2_conv_in["A_logs"],
        "L2_conv_Ds": _L2_conv_in["Ds"],
        "L2_conv_ln_gamma": _L2_conv_in["ln_gamma"],
        "L2_conv_ln_beta": _L2_conv_in["ln_beta"],
        "L2_conv_out_proj_w": _L2_conv_in["out_proj_w"],
        "L3_conv_in_proj_w": _L3_conv_in["in_proj_w"],
        "L3_conv_conv_w": _L3_conv_in["conv_w"],
        "L3_conv_conv_b": _L3_conv_in["conv_b"],
        "L3_conv_x_proj_weight": _L3_conv_in["x_proj_weight"],
        "L3_conv_dt_projs_weight": _L3_conv_in["dt_projs_weight"],
        "L3_conv_dt_projs_bias": _L3_conv_in["dt_projs_bias"],
        "L3_conv_A_logs": _L3_conv_in["A_logs"],
        "L3_conv_Ds": _L3_conv_in["Ds"],
        "L3_conv_ln_gamma": _L3_conv_in["ln_gamma"],
        "L3_conv_ln_beta": _L3_conv_in["ln_beta"],
        "L3_conv_out_proj_w": _L3_conv_in["out_proj_w"],
    }

def reference(x, L0_conv_in_proj_w, L0_conv_conv_w, L0_conv_conv_b, L0_conv_x_proj_w, L0_conv_dt_projs_w, L0_conv_A_logs, L0_conv_Ds, L0_conv_dt_projs_bias, L0_conv_norm_w, L0_conv_norm_b, L0_conv_out_proj_w, L1_conv_in_proj_w, L1_conv_conv_w, L1_conv_conv_b, L1_conv_x_proj_weight, L1_conv_dt_projs_weight, L1_conv_dt_projs_bias, L1_conv_A_logs, L1_conv_Ds, L1_conv_direction_Bs, L1_conv_pf_w1, L1_conv_pf_b1, L1_conv_pf_w2, L1_conv_pf_b2, L1_conv_ln_g, L1_conv_ln_b, L1_conv_out_proj_w, L2_conv_in_proj_w, L2_conv_conv_w, L2_conv_conv_b, L2_conv_x_proj_weight, L2_conv_dt_projs_weight, L2_conv_dt_projs_bias, L2_conv_A_logs, L2_conv_Ds, L2_conv_ln_gamma, L2_conv_ln_beta, L2_conv_out_proj_w, L3_conv_in_proj_w, L3_conv_conv_w, L3_conv_conv_b, L3_conv_x_proj_weight, L3_conv_dt_projs_weight, L3_conv_dt_projs_bias, L3_conv_A_logs, L3_conv_Ds, L3_conv_ln_gamma, L3_conv_ln_beta, L3_conv_out_proj_w):
    import jax
    import jax.numpy as jnp
    def _L0_conv_ref(x, in_proj_w, conv_w, conv_b, x_proj_w, dt_projs_w, A_logs, Ds, dt_projs_bias, norm_w, norm_b, out_proj_w):
        import jax, jax.numpy as jnp
        import numpy as np
        B, H, W = (8, 64, 64)
        D_MODEL, D_STATE, D_INNER, DT_RANK, K = (96, 16, 192, 6, 4)
        EPS = 1e-06

        def _ss2d(x, in_proj_w, conv_w, conv_b, x_proj_w, dt_projs_w, A_logs, Ds, dt_projs_bias, norm_w, norm_b, out_proj_w):
            silu = jax.nn.silu
            Bb, Hh, Ww, _ = x.shape
            L = Hh * Ww
            xz = x @ in_proj_w.T
            xx, z = jnp.split(xz, 2, axis=-1)
            z = silu(z)
            xc = jnp.transpose(xx, (0, 3, 1, 2))
            xc = jax.lax.conv_general_dilated(xc, conv_w, (1, 1), ((1, 1), (1, 1)), dimension_numbers=('NCHW', 'OIHW', 'NCHW'), feature_group_count=D_INNER) + conv_b[None, :, None, None]
            xc = silu(xc)
            x_hw = xc.reshape(Bb, D_INNER, L)
            x_wh = jnp.transpose(xc, (0, 1, 3, 2)).reshape(Bb, D_INNER, L)
            xs = jnp.stack([x_hw, x_wh, x_hw[..., ::-1], x_wh[..., ::-1]], axis=1)
            xpw = x_proj_w.reshape(K, DT_RANK + 2 * D_STATE, D_INNER)
            x_dbl = jnp.einsum('bkdl,kcd->bkcl', xs, xpw)
            dts, Bs, Cs = jnp.split(x_dbl, [DT_RANK, DT_RANK + D_STATE], axis=2)
            dtw = dt_projs_w.reshape(K, D_INNER, DT_RANK)
            dts = jnp.einsum('bkrl,kdr->bkdl', dts, dtw)
            A = -jnp.exp(A_logs).reshape(K, D_INNER, D_STATE)
            dt = jax.nn.softplus(dts + dt_projs_bias.reshape(1, K, D_INNER, 1))

            def step(h, inp):
                u_t, dt_t, B_t, C_t = inp
                dA = jnp.exp(dt_t[..., None] * A)
                h = h * dA + (dt_t * u_t)[..., None] * B_t[:, :, None, :]
                y = jnp.einsum('bkdn,bkn->bkd', h, C_t)
                return (h, y)
            h0 = jnp.zeros((Bb, K, D_INNER, D_STATE), jnp.float32)
            seq = (jnp.moveaxis(xs, -1, 0), jnp.moveaxis(dt, -1, 0), jnp.moveaxis(Bs, -1, 0), jnp.moveaxis(Cs, -1, 0))
            _, ysL = jax.lax.scan(step, h0, seq)
            ys = jnp.moveaxis(ysL, 0, -1)
            ys = ys + xs * Ds.reshape(1, K, D_INNER, 1)
            y = ys[:, 0] + ys[:, 2][..., ::-1]
            yw = ys[:, 1] + ys[:, 3][..., ::-1]
            y = y + yw.reshape(Bb, D_INNER, Ww, Hh).transpose(0, 1, 3, 2).reshape(Bb, D_INNER, L)
            y = y.reshape(Bb, D_INNER, Hh, Ww).transpose(0, 2, 3, 1)
            mean = y.mean(-1, keepdims=True)
            var = ((y - mean) ** 2).mean(-1, keepdims=True)
            y = (y - mean) / jnp.sqrt(var + EPS) * norm_w + norm_b
            y = y * z
            return y @ out_proj_w.T
        return _ss2d(x, in_proj_w, conv_w, conv_b, x_proj_w, dt_projs_w, A_logs, Ds, dt_projs_bias, norm_w, norm_b, out_proj_w)

    def _L1_conv_ref(x, in_proj_w, conv_w, conv_b, x_proj_weight, dt_projs_weight, dt_projs_bias, A_logs, Ds, direction_Bs, pf_w1, pf_b1, pf_w2, pf_b2, ln_g, ln_b, out_proj_w):
        import math
        import jax, jax.numpy as jnp
        import numpy as np
        B_, H_, W_, D_MODEL = (4, 64, 64, 96)
        D_STATE, D_CONV, EXPAND, K_ = (16, 3, 2, 4)
        D_INNER = EXPAND * D_MODEL
        DT_RANK = math.ceil(D_MODEL / 16)

        def _scan_indices(H, W):
            L = H * W
            o1 = []
            for s in range(H + W - 1):
                coords = [i * W + (s - i) for i in range(max(0, s - W + 1), min(H, s + 1))]
                if s % 2 == 1:
                    coords = coords[::-1]
                o1.extend(coords)
            o2 = []
            for s in range(H + W - 1):
                coords = []
                for i in range(max(0, s - W + 1), min(H, s + 1)):
                    j = W - 1 - (s - i)
                    if 0 <= j < W:
                        coords.append(i * W + j)
                if s % 2 == 1:
                    coords = coords[::-1]
                o2.extend(coords)
            cy, cx = (H // 2, W // 2)
            yy, xx = np.meshgrid(np.arange(H), np.arange(W), indexing='ij')
            dy, dx = (yy - cy, xx - cx)
            r = np.sqrt(dy ** 2 + dx ** 2)
            th = np.arctan2(dy, dx)
            o3 = np.argsort((r * (L + 1) + (th + np.pi) * 10).flatten())
            o4 = np.argsort((-r * (L + 1) + (th + np.pi) * 10).flatten())
            idx = np.stack([np.array(o1), np.array(o2), o3, o4]).astype(np.int32)
            inv = np.argsort(idx, axis=1).astype(np.int32)
            return (idx, inv)
        B, H, W, C = x.shape
        L = H * W
        K, d_state = direction_Bs.shape
        d_inner = conv_w.shape[0]
        dt_rank = dt_projs_weight.shape[2]
        xz = x @ in_proj_w.T
        xc, z = jnp.split(xz, 2, axis=-1)
        xc = jnp.transpose(xc, (0, 3, 1, 2))
        xc = jax.lax.conv_general_dilated(xc, conv_w, (1, 1), 'SAME', feature_group_count=d_inner, dimension_numbers=('NCHW', 'OIHW', 'NCHW')) + conv_b[None, :, None, None]
        xc = jax.nn.silu(xc)
        idx, inv = _scan_indices(H, W)
        x_flat = xc.reshape(B, d_inner, L)
        xs = jnp.stack([x_flat[:, :, idx[k]] for k in range(K)], axis=1)
        x_dbl = jnp.einsum('bkdl,kcd->bkcl', xs, x_proj_weight)
        dts = x_dbl[:, :, :dt_rank]
        Bs = x_dbl[:, :, dt_rank:dt_rank + d_state]
        Cs = x_dbl[:, :, dt_rank + d_state:]
        dts = jnp.einsum('bkrl,kdr->bkdl', dts, dt_projs_weight)
        Bs = Bs + direction_Bs[None, :, :, None]
        A = -jnp.exp(A_logs).reshape(K, d_inner, d_state)
        delta = jax.nn.softplus(dts + dt_projs_bias.reshape(K, d_inner)[None, :, :, None])
        dt_t = jnp.moveaxis(delta, -1, 0)
        u_t = jnp.moveaxis(xs, -1, 0)
        B_t = jnp.moveaxis(Bs, -1, 0)
        C_t = jnp.moveaxis(Cs, -1, 0)

        def step(h, inp):
            dt, u, Bl, Cl = inp
            h = h * jnp.exp(dt[..., None] * A) + (dt * u)[..., None] * Bl[:, :, None, :]
            y = jnp.einsum('bkdn,bkn->bkd', h, Cl)
            return (h, y)
        h0 = jnp.zeros((B, K, d_inner, d_state), x.dtype)
        _, ys = jax.lax.scan(step, h0, (dt_t, u_t, B_t, C_t))
        out_y = jnp.moveaxis(ys, 0, -1) + Ds.reshape(K, d_inner)[None, :, :, None] * xs
        y_restored = jnp.stack([out_y[:, k][:, :, inv[k]] for k in range(K)], axis=1)
        cy, cx = (H / 2.0, W / 2.0)
        yy, xx = jnp.meshgrid(jnp.arange(H, dtype=x.dtype), jnp.arange(W, dtype=x.dtype), indexing='ij')
        dy = (yy - cy) / (H / 2.0)
        dx = (xx - cx) / (W / 2.0)
        r = jnp.clip(jnp.sqrt(dy ** 2 + dx ** 2), None, 2.0)
        th = jnp.arctan2(dy, dx) / math.pi
        coords = jnp.stack([r, th], -1).reshape(L, 2)
        w = jax.nn.gelu(coords @ pf_w1.T + pf_b1, approximate=False) @ pf_w2.T + pf_b2
        w = jax.nn.softmax(w, axis=-1)
        y_fused = jnp.einsum('bkdl,lk->bdl', y_restored, w)
        y = jnp.transpose(y_fused, (0, 2, 1)).reshape(B, H, W, d_inner)
        mu = jnp.mean(y, -1, keepdims=True)
        var = jnp.var(y, -1, keepdims=True)
        y = (y - mu) / jnp.sqrt(var + 1e-05) * ln_g + ln_b
        y = y * jax.nn.silu(z)
        return y @ out_proj_w.T

    def _L2_conv_ref(x, in_proj_w, conv_w, conv_b, x_proj_weight, dt_projs_weight, dt_projs_bias, A_logs, Ds, ln_gamma, ln_beta, out_proj_w):
        import math
        import jax, jax.numpy as jnp
        import numpy as np
        D_MODEL = 96
        D_STATE = 16
        D_CONV = 3
        EXPAND = 2
        D_INNER = EXPAND * D_MODEL
        DT_RANK = math.ceil(D_MODEL / 16)
        K = 4
        BATCH = 2
        HH = 64
        WW = 64

        def _selective_scan(u, delta, A, Bm, Cm, D, delta_bias):
            delta = jax.nn.softplus(delta + delta_bias[None, :, :, None])
            dL = jnp.moveaxis(delta, -1, 0)
            uL = jnp.moveaxis(u, -1, 0)
            BL = jnp.moveaxis(Bm, -1, 0)
            CL = jnp.moveaxis(Cm, -1, 0)
            Bsz, Kk, Dn, L = u.shape
            N = A.shape[-1]
            x0 = jnp.zeros((Bsz, Kk, Dn, N), dtype=u.dtype)

            def step(xstate, inp):
                d_l, u_l, b_l, c_l = inp
                dA = jnp.exp(d_l[..., None] * A)
                dBu = d_l[..., None] * b_l[:, None] * u_l[..., None]
                xstate = dA * xstate + dBu
                y = jnp.einsum('bkdn,bdn->bkd', xstate, c_l)
                return (xstate, y)
            _, ys = jax.lax.scan(step, x0, (dL, uL, BL, CL))
            y = jnp.moveaxis(ys, 0, -1)
            return y + u * D[None, :, :, None]
        B, H, W, C = x.shape
        Dn = conv_w.shape[0]
        N = A_logs.shape[-1]
        R = dt_projs_weight.shape[-1]
        L = H * W
        xz = x @ in_proj_w.T
        xx, z = jnp.split(xz, 2, axis=-1)
        xc = jnp.transpose(xx, (0, 3, 1, 2))
        pad = (conv_w.shape[-1] - 1) // 2
        xc = jax.lax.conv_general_dilated(xc, conv_w, (1, 1), [(pad, pad), (pad, pad)], dimension_numbers=('NCHW', 'OIHW', 'NCHW'), feature_group_count=Dn) + conv_b[None, :, None, None]
        xc = jax.nn.silu(xc)
        x_flat = xc.reshape(B, Dn, L)
        x_wh = jnp.transpose(xc, (0, 1, 3, 2)).reshape(B, Dn, L)
        x_hwwh = jnp.stack([x_flat, x_wh], axis=1)
        xs = jnp.concatenate([x_hwwh, jnp.flip(x_hwwh, axis=-1)], axis=1)
        x_dbl = jnp.einsum('bkdl,kcd->bkcl', xs, x_proj_weight)
        dts = x_dbl[:, :, :R]
        Bs = x_dbl[:, :, R:R + N]
        Cs = x_dbl[:, :, R + N:]
        dts = jnp.einsum('bkrl,kdr->bkdl', dts, dt_projs_weight)
        A = -jnp.exp(A_logs).reshape(K, Dn, N)
        gidx = jnp.arange(Dn) % K
        Bm = Bs[:, gidx]
        Cm = Cs[:, gidx]
        out_y = _selective_scan(xs, dts, A, Bm, Cm, Ds.reshape(K, Dn), dt_projs_bias)
        inv_y = jnp.flip(out_y[:, 2:4], axis=-1)
        wh_y = jnp.transpose(out_y[:, 1].reshape(B, Dn, W, H), (0, 1, 3, 2)).reshape(B, Dn, L)
        invwh_y = jnp.transpose(inv_y[:, 1].reshape(B, Dn, W, H), (0, 1, 3, 2)).reshape(B, Dn, L)
        y = out_y[:, 0] + inv_y[:, 0] + wh_y + invwh_y
        y = jnp.transpose(y, (0, 2, 1)).reshape(B, H, W, Dn)
        mu = y.mean(-1, keepdims=True)
        var = y.var(-1, keepdims=True)
        y = (y - mu) / jnp.sqrt(var + 1e-05) * ln_gamma + ln_beta
        y = y * jax.nn.silu(z)
        return y @ out_proj_w.T

    def _L3_conv_ref(x, in_proj_w, conv_w, conv_b, x_proj_weight, dt_projs_weight, dt_projs_bias, A_logs, Ds, ln_gamma, ln_beta, out_proj_w):
        import jax, jax.numpy as jnp
        import numpy as np
        import math
        B_, H_, W_, DM, DE, K_, N_, R_ = (2, 48, 48, 96, 192, 4, 16, 6)

        def _ss2d(x, in_proj_w, conv_w, conv_b, x_proj_weight, dt_projs_weight, dt_projs_bias, A_logs, Ds, ln_gamma, ln_beta, out_proj_w):
            B, H, W, _ = x.shape
            DE = conv_w.shape[0]
            K = x_proj_weight.shape[0]
            N = A_logs.shape[1]
            R = dt_projs_weight.shape[2]
            L = H * W
            xz = jnp.einsum('bhwc,dc->bhwd', x, in_proj_w)
            xh, z = jnp.split(xz, 2, axis=-1)
            z = jax.nn.silu(z)
            xc = jnp.transpose(xh, (0, 3, 1, 2))
            xc = jax.lax.conv_general_dilated(xc, conv_w, (1, 1), 'SAME', dimension_numbers=('NCHW', 'OIHW', 'NCHW'), feature_group_count=DE)
            xc = jax.nn.silu(xc + conv_b[None, :, None, None])
            x_hs = xc.reshape(B, DE, L)
            x_vs = jnp.swapaxes(xc, 2, 3).reshape(B, DE, L)
            xs = jnp.stack([x_hs, x_hs[..., ::-1], x_vs, x_vs[..., ::-1]], axis=1)
            x_dbl = jnp.einsum('bkdl,kcd->bkcl', xs, x_proj_weight)
            dts = x_dbl[:, :, :R]
            Bs = x_dbl[:, :, R:R + N]
            Cs = x_dbl[:, :, R + N:]
            dts = jnp.einsum('bkrl,kdr->bkdl', dts, dt_projs_weight)
            delta = jax.nn.softplus(dts + dt_projs_bias[None, :, :, None])
            A = -jnp.exp(A_logs).reshape(K, DE, N)
            dA = jnp.exp(delta[..., None] * A[None, :, :, None, :])
            dBu = (delta * xs)[..., None] * jnp.swapaxes(Bs, 2, 3)[:, :, None]

            def comb(e1, e2):
                a1, b1 = e1
                a2, b2 = e2
                return (a2 * a1, a2 * b1 + b2)
            _, hstate = jax.lax.associative_scan(comb, (dA, dBu), axis=3)
            ys = jnp.einsum('bkdln,bknl->bkdl', hstate, Cs) + Ds.reshape(K, DE)[None, :, :, None] * xs

            def rev_v(y):
                return jnp.swapaxes(y.reshape(B, DE, W, H), 2, 3).reshape(B, DE, L)
            y = ys[:, 0] + ys[:, 1, :, ::-1] + rev_v(ys[:, 2]) + rev_v(ys[:, 3, :, ::-1])
            y = jnp.swapaxes(y, 1, 2)
            mu = jnp.mean(y, axis=-1, keepdims=True)
            var = jnp.mean(jnp.square(y - mu), axis=-1, keepdims=True)
            y = (y - mu) * jax.lax.rsqrt(var + 1e-05) * ln_gamma + ln_beta
            y = y.reshape(B, H, W, DE).astype(x.dtype)
            return jnp.einsum('bhwd,cd->bhwc', y * z, out_proj_w)
        return _ss2d(x, in_proj_w, conv_w, conv_b, x_proj_weight, dt_projs_weight, dt_projs_bias, A_logs, Ds, ln_gamma, ln_beta, out_proj_w)

    def _gn(v, G=32, eps=1e-5):
        B_, H_, W_, C_ = v.shape
        g = v.reshape(B_, H_, W_, G, C_ // G)
        m = jnp.mean(g, axis=(1, 2, 4), keepdims=True)
        s = jnp.var(g, axis=(1, 2, 4), keepdims=True)
        return ((g - m) / jnp.sqrt(s + eps)).reshape(v.shape)

    def _ln_c(v, eps=1e-6):
        m = jnp.mean(v, axis=-1, keepdims=True)
        s = jnp.var(v, axis=-1, keepdims=True)
        return (v - m) / jnp.sqrt(s + eps)

    def _ln_t(v, eps=1e-5):
        m = jnp.mean(v, axis=-1, keepdims=True)
        s = jnp.var(v, axis=-1, keepdims=True)
        return (v - m) / jnp.sqrt(s + eps)

    def _to_tokens(v):
        B_, H_, W_, C_ = v.shape
        return v.reshape(B_, H_ * W_, C_)
    def _from_tokens(t, like):
        return t.reshape(like.shape)

    x = x + _L0_conv_ref(_gn(x), L0_conv_in_proj_w, L0_conv_conv_w, L0_conv_conv_b, L0_conv_x_proj_w, L0_conv_dt_projs_w, L0_conv_A_logs, L0_conv_Ds, L0_conv_dt_projs_bias, L0_conv_norm_w, L0_conv_norm_b, L0_conv_out_proj_w)
    x = x + _L1_conv_ref(_gn(x), L1_conv_in_proj_w, L1_conv_conv_w, L1_conv_conv_b, L1_conv_x_proj_weight, L1_conv_dt_projs_weight, L1_conv_dt_projs_bias, L1_conv_A_logs, L1_conv_Ds, L1_conv_direction_Bs, L1_conv_pf_w1, L1_conv_pf_b1, L1_conv_pf_w2, L1_conv_pf_b2, L1_conv_ln_g, L1_conv_ln_b, L1_conv_out_proj_w)
    x = x + _L2_conv_ref(_gn(x), L2_conv_in_proj_w, L2_conv_conv_w, L2_conv_conv_b, L2_conv_x_proj_weight, L2_conv_dt_projs_weight, L2_conv_dt_projs_bias, L2_conv_A_logs, L2_conv_Ds, L2_conv_ln_gamma, L2_conv_ln_beta, L2_conv_out_proj_w)
    x = x + _L3_conv_ref(_gn(x), L3_conv_in_proj_w, L3_conv_conv_w, L3_conv_conv_b, L3_conv_x_proj_weight, L3_conv_dt_projs_weight, L3_conv_dt_projs_bias, L3_conv_A_logs, L3_conv_Ds, L3_conv_ln_gamma, L3_conv_ln_beta, L3_conv_out_proj_w)
    return x


_drawn_inputs = setup_inputs


def setup_inputs(seed=0):
    import zlib

    import numpy as np

    out = dict(_drawn_inputs(seed))
    spreads = {'L0_conv_conv_b': (0.0, 0.1),
     'L0_conv_Ds': (1.0, 0.6),
     'L0_conv_norm_w': (1.0, 0.6),
     'L0_conv_norm_b': (0.0, 0.8),
     'L1_conv_conv_b': (0.0, 0.1),
     'L1_conv_Ds': (1.0, 0.6),
     'L1_conv_pf_b1': (0.0, 0.8),
     'L1_conv_pf_b2': (0.0, 0.8),
     'L1_conv_ln_g': (1.0, 0.6),
     'L1_conv_ln_b': (0.0, 0.8),
     'L2_conv_conv_b': (0.0, 0.1),
     'L2_conv_Ds': (1.0, 0.2),
     'L2_conv_ln_gamma': (1.0, 0.2),
     'L2_conv_ln_beta': (0.0, 0.1),
     'L3_conv_conv_b': (0.0, 0.1),
     'L3_conv_Ds': (1.0, 0.2),
     'L3_conv_ln_gamma': (1.0, 0.2),
     'L3_conv_ln_beta': (0.0, 0.1)}
    factors = {'L0_conv_conv_w': 2.745,
     'L0_conv_x_proj_w': 8.0,
     'L0_conv_dt_projs_w': 8.0,
     'L0_conv_A_logs': 8.0,
     'L0_conv_dt_projs_bias': 8.0,
     'L1_conv_conv_w': 2.859,
     'L1_conv_x_proj_weight': 8.0,
     'L1_conv_dt_projs_weight': 8.0,
     'L1_conv_dt_projs_bias': 8.0,
     'L1_conv_A_logs': 8.0,
     'L1_conv_direction_Bs': 8.0,
     'L1_conv_pf_w1': 8.0,
     'L1_conv_pf_w2': 8.0,
     'L2_conv_dt_projs_weight': 6.977,
     'L2_conv_dt_projs_bias': 3.497,
     'L2_conv_A_logs': 4.812,
     'L3_conv_dt_projs_weight': 3.806,
     'L3_conv_dt_projs_bias': 3.666,
     'L3_conv_A_logs': 6.237}
    for name, (base, spread) in spreads.items():
        noise = np.random.default_rng([zlib.crc32(name.encode()), seed]).standard_normal(out[name].shape)
        drawn = base * np.exp(spread * noise) if base else spread * noise
        out[name] = jnp.asarray(drawn.astype(out[name].dtype))
    for name, factor in factors.items():
        out[name] = (out[name] * factor).astype(out[name].dtype)
    return out
```

```python
from contextlib import ExitStack

import numpy as np

import concourse.bass as bass
from concourse import mybir

ALU = mybir.AluOpType
ACT = mybir.ActivationFunctionType
AX_X = mybir.AxisListType.X
F32 = mybir.dt.float32
F32R = mybir.dt.float32r
U32 = mybir.dt.uint32

P = 128
HH = WW = 64
L = HH * WW
DM = 96
DI = 192
DB = DI - P
K = 4
N = 16
R = 6
XD = R + 2 * N
G8 = P // N
UN = DI // G8
UA = P // G8
CH = 1024
NC = L // CH
SL = 512
NS = L // SL
BLK = L // P
RDA = 4
RH = 8
LEAD = 5
CREDIT = 32
PADW = WW + 2

LAYERS = [
    dict(name="L0_conv", xproj="x_proj_w", dtw="dt_projs_w", g="norm_w", b="norm_b", eps=1e-6, dirs=["n", "w", "rn", "rw"]),
    dict(name="L1_conv", xproj="x_proj_weight", dtw="dt_projs_weight", g="ln_g", b="ln_b", eps=1e-5, dirs=["g"] * 4),
    dict(name="L2_conv", xproj="x_proj_weight", dtw="dt_projs_weight", g="ln_gamma", b="ln_beta", eps=1e-5, dirs=["n", "w", "rn", "rw"]),
    dict(name="L3_conv", xproj="x_proj_weight", dtw="dt_projs_weight", g="ln_gamma", b="ln_beta", eps=1e-5, dirs=["n", "rn", "w", "rw"]),
]


def unit_place(t):
    if t < UA:
        return True, t % 4, t // 4
    return False, (t - UA) % 2, (t - UA) // 2


def ordered(ap, kind):
    if "r" in kind:
        ap = ap[:, ::-1]
    if "w" in kind:
        return ap.rearrange("p (h w) -> p w h", w=WW)
    return ap.rearrange("p (h w) -> p h w", w=WW)


def build(nc, B, layers, t_in, out):
    ctx = ExitStack()
    with ctx:
        def sb(name, shape, dt=F32):
            return ctx.enter_context(nc.sbuf_tensor(name, shape, dt))

        def sem(name):
            return ctx.enter_context(nc.semaphore(name))

        def dram(name, shape):
            return nc.dram_tensor(name, shape, F32, kind="Internal").ap()

        stream = [dram(f"stream{i}", [B, DM, L]) for i in range(len(layers) - 1)]
        xs_d = dram("xs_by_direction", [K, DI, L])
        xd_d = dram("xproj_by_direction", [K, XD, L])
        y_d = dram("y_by_direction", [K, DI, L])
        xtok_d = dram("x_tokens", [L, DI])
        ytok_d = [dram(f"y_tokens{k}", [L, DI]) for k in range(K)]

        xn = sb("xn_padded", [DM, PADW * PADW])
        xn_img = xn[:].rearrange("p (h w) -> p h w", w=PADW)
        w_in = sb("w_in", [DM, 2 * DI])
        w_conv = sb("w_conv", [DM, 9 * DI])
        w_xpA = sb("w_xprojA", [P, K * XD])
        w_xpB = sb("w_xprojB", [DB, K * XD])
        w_dt = sb("w_dt", [P, K * DI])
        rank = sb("rank", [P, CH])[:]
        a_neg = sb("a_neg", [P, K * UN])
        vecA = sb("channel_vectorsA", [P, 16])
        vecB = sb("channel_vectorsB", [DB, 16])
        V_D, V_DTB, V_CB, V_G, V_B = 0, 4, 8, 9, 10
        w_outA = sb("w_outA", [P, DM])
        w_outB = sb("w_outB", [DB, DM])
        ident = sb("identity", [P, P])
        spread_r = sb("spread", [P, 4 * 4 * P], F32R)
        gather8 = sb("gather8", [P, 4 * 32])
        mean192 = sb("mean192", [P, P])
        mean3 = sb("mean3", [DM, DM])
        carry = sb("carry", [P, K * UN])
        gn_s = sb("gn_statistics", [DM, 6 * NS])
        gn_v = sb("gn_values", [DM, 16])
        dir_b = sb("direction_bias", [XD, K])
        order = sb("order", [P, K * BLK], U32)
        w_pos = sb("w_pos", [P, K * BLK])
        pf = sb("pf_weights", [P, 64])

        with nc.sbuf_tensor("split_parts", [P, 12 * CH], F32R) as parts:
            pass
        arena = sb("arena", [P, 38912])
        at = [0]

        def place(n, start=None):
            if start is not None:
                at[0] = start
            a = arena[:, at[0]:at[0] + n]
            at[0] += n
            return a

        xsA = [place(CH, 12 * CH), place(CH)]
        xsB = [place(CH), place(CH)]
        bt = [place(CH), place(CH)]
        ct = [place(CH), place(CH)]
        hi = {}
        lo = {}
        for tile in ("dtA", "duA", "mixB"):
            hi[tile] = [parts[:, (4 * len(hi) + i) * CH:(4 * len(hi) + i + 1) * CH] for i in range(2)]
            lo[tile] = [parts[:, (4 * len(lo) + 2 + i) * CH:(4 * len(lo) + 3 + i) * CH] for i in range(2)]
        rz, az = (place(CH), sb("rzB", [P, CH])[:]), (place(CH), sb("azB", [P, CH])[:])
        wz, lz = place(CH), place(CH)
        decay = [place(CH) for _ in range(RDA)]
        state = [place(CH) for _ in range(RH)]
        yoA, yoB = place(CH), place(CH)
        assert at[0] == 38912 - 0
        xcA, xcB = place(L, 0), place(L)
        permA, permB = zip(*[(place(L), place(L)) for _ in range(2)])
        xdt = [place(L), place(L)]
        x_in = place(L)
        tok_g = place(BLK * DI, 32768)
        tok_x = place(BLK * DI, 4 * L)
        zsA, zsB = place(L, 0), place(L)
        yA = [place(L) for _ in range(4)]
        yB = [place(L)] + yA[1:]
        sq = [place(2 * SL) for _ in range(2)]
        rs = [place(SL) for _ in range(3)]
        xres = [place(SL) for _ in range(2)]
        xout = [place(SL) for _ in range(2)]
        yin = [(place(L, 0), place(L)), (place(L), place(L))]
        tok_o = [place(BLK * DI), place(BLK * DI)]
        ytok = [place(BLK * DI, 2 * L)] + [place(BLK * DI) for _ in range(K - 1)]
        y_sum = place(L, 2 * L + BLK * DI), place(L)
        spread = place(4 * 4 * P, 0)
        cw_rows = place(9 * DI, 2048)
        coords = place(K * L, 4096)
        hid = [place(SL), place(SL)]
        logit = [place(4 * P) for _ in range(3)]
        red = [place(P) for _ in range(3)]

        ps = ctx.enter_context(nc.psum_tensor("banks", [P, 8, 512], F32))

        def bank(i, rows=P, cols=512, row0=0):
            return ps[row0:row0 + rows, i, 0:cols]

        ps_dt = ps[:, 0:2, :].rearrange("p a b -> p (a b)")
        ps_du = [ps[:, 2 + 2 * i:4 + 2 * i, :].rearrange("p a b -> p (a b)") for i in range(2)]
        ps_y = ps[:, 6:8, :].rearrange("p a b -> p (a b)")

        class Count:

            def __init__(self, c, m, k):
                self.c, self.m, self.k = (c, m, k) if not isinstance(c, int) else (None, 0, c * m + k)

            def __add__(self, n):
                return Count(self.c, self.m, self.k + n) if self.c is not None else Count(0, 0, self.k + n)

            def __sub__(self, n):
                return self + -n

            def __mul__(self, n):
                return Count(self.c, self.m * n, self.k * n) if self.c is not None else Count(0, 0, self.k * n)

        class Signal:

            def __init__(self, name, per, credit=CREDIT):
                self.h, self.per, self.credit = sem(name), per, credit

            def at(self, gb, n):
                b, g0 = gb
                n = n if isinstance(n, Count) else Count(0, 0, n)
                v = g0 * self.per + n.k + self.credit
                assert v >= 0
                if n.c is not None:
                    v = n.c * n.m + v
                return v if isinstance(b, int) else b * self.per + v

        CHK = K * NC
        const_in = sem("const_in")
        const_ok = sem("const_ok")
        wts_in = sem("wts_in")
        wts_ok = sem("wts_ok")
        init_dve = sem("init_dve")
        setup_dve = sem("setup_dve")
        setup_exp = sem("setup_exp")
        setup_pe = sem("setup_pe")
        setup_act = sem("setup_act")
        step_done = {e: sem(f"step_done_{n}") for e, n in ((nc.vector, "dve"), (nc.tensor, "pe"), (nc.gpsimd, "pool"), (nc.sync, "sp"))}
        x_ld = Signal("x_loaded", 16, 0)
        gn_dve = Signal("gn_dve", 13)
        gn_pe = Signal("gn_grouped", 2)
        gn_act = Signal("gn_act", 2)
        cv_pe = Signal("conv_summed", 2 * NS)
        cv_act = Signal("conv_active", 2 * NS)
        pm_dve = Signal("orderA", K)
        pm_act = Signal("orderB", K)
        xp_pe = Signal("xproj_summed", K * NS)
        xp_dve = Signal("xproj_copied", K * NS)
        pre_st = [Signal(f"pre_stored{i}", 2 * 48, 0) for i in range(2)]
        ld_all = [Signal(f"chunk_loaded{i}", CHK // 2 * 64, 0) for i in range(2)]
        ld_mix = [Signal(f"chunk_loaded_mixed{i}", CHK // 2 * (2 + 2 * K) * 16, 0) for i in range(2)]
        ld_r = Signal("rank_loaded", CHK * 16, 0)
        dt_f = Signal("dt_spread", CHK * UN)
        du_f = Signal("du_spread", CHK * UN)
        ex = Signal("decay_ready", CHK * UN)
        dbu = Signal("dbu_ready", CHK * UN)
        sc = Signal("scanned", CHK * UN)
        ca = Signal("carry_kept", CHK * UN)
        pr = Signal("times_c", CHK * UN)
        yq = Signal("y_summed", CHK * 6)
        ev = Signal("y_out", CHK * 2)
        stA = Signal("yA_stored", CHK * 16, 0)
        stB = Signal("yB_stored", CHK * 16, 0)
        z_pe = Signal("z_ready", CHK * 2)
        z_act = Signal("z_taken", CHK * 2)
        sp_a = Signal("softplus_abs", CHK * 2)
        sp_e = Signal("softplus_exp", CHK * 2)
        sp_w = Signal("softplus_one_plus", CHK * 2)
        sp_l = Signal("softplus_log", CHK * 2)
        sp_r = Signal("softplus_rest", CHK * 2)
        sp_s = Signal("softplus_partial", CHK * 2)
        dt_ok = Signal("dt_ready", CHK * 2)
        du_ok = Signal("du_ready", CHK * 2)
        hi_ok = Signal("hi_ready", CHK * 3)
        lo_ok = Signal("lo_ready", CHK * 3)
        cz = Signal("carry_zeroed", 1)
        y_ld = [Signal(f"y_loaded{i}", 64, 0) for i in range(2)]
        cb = Signal("directions_added", 6)
        zz_pe = Signal("gate_summed", 2 * NS)
        zz_act = Signal("gate_ready", 2 * NS)
        mu_pe = Signal("mean_ready", NS)
        yc = Signal("y_centred", NS)
        sq_act = Signal("squares_ready", NS)
        va_pe = Signal("variance_ready", NS)
        ln_act = Signal("log_variance", NS)
        rs_act = Signal("rstd_ready", NS)
        yn = Signal("y_normed", NS)
        af = Signal("y_affine", NS)
        gt = Signal("y_gated", NS)
        op_pe = Signal("out_projected", NS)
        xo = Signal("x_out", NS)
        xr_ld = [Signal(f"residual_loaded{i}", NS // 2 * 16, 0) for i in range(2)]
        xo_st = [Signal(f"x_stored{i}", NS // 2 * 16, 0) for i in range(2)]
        tk_pe = Signal("tokens_turned", BLK // 2)
        tk_cp = Signal("tokens_copied", BLK // 2)
        tk_st = Signal("tokens_stored", 16, 0)
        tg = Signal("tokens_gathered", K * BLK * 16, 0)
        pm_cpA = Signal("gatheredA_copied", K * NS)
        pm_cpB = Signal("gatheredB_copied", K * NS)
        ga_pe = Signal("gatheredA_turned", K * NS)
        gb_pe = Signal("gatheredB_turned", K * NS)
        yt_ld = [Signal(f"scan_y_loaded{i}", 2 * 32, 0) for i in range(2)]
        yt_pe = Signal("y_tokens_turned", K * BLK // 2)
        yt_act = Signal("y_tokens_weighted", K * BLK // 2)
        ys_st = [Signal(f"y_tokens_stored{i}", K // 2 * BLK * 16, 0) for i in range(2)]
        yr_ld = Signal("y_tokens_loaded", K * 16, 0)
        yr_ad = Signal("y_tokens_added", 3)
        yb_pe = Signal("y_turned_back", 2 * NS)
        yb_cp = Signal("y_back", 2 * NS)

        block = ctx.enter_context(nc.Block())
        is_tab = [s["dirs"][0] == "g" for s in layers]
        mixed = [s["name"] == "L2_conv" for s in layers]
        counts = [sum(24 if q else 18 for q in is_tab[:i + 1]) for i in range(len(layers))]
        ready = [sum(2 + K if q else 2 for q in is_tab[:i + 1]) for i in range(len(layers))]

        def post_y(tab):
            return y_sum if tab else (yA[0], yB[0])

        def ln_eps(li, rows=P):
            return vecA[0:rows, 11:12] if layers[li]["eps"] == 1e-6 else vecA[0:rows, 12:13]

        def per_layer():
            for i, spec in enumerate(layers):
                yield i, spec, i * B, spec["dirs"][0] == "g"

        def loaded(eng, li, b, c, k):
            s, one = (ld_mix, (2 + 2 * K) * 16) if mixed[li] else (ld_all, 64)
            alike = sum(q == mixed[li] for q in mixed[:li])
            eng.wait_ge(s[k % 2].h, s[k % 2].at((b, alike * B), Count(c, 2 * one, (k // 2 + 1) * one)))

        def nxt(c, k):
            return (c, k + 1) if k < K - 1 else (c + 1, 0)

        def chunks(eng, body):
            with eng.Fori(0, NC - 1) as c:
                for k in range(K):
                    body(c, k, False)
            for k in range(K):
                body(NC - 1, k, k == K - 1)

        def uno(c, k, t):
            return Count(c, K * UN, k * UN + t)

        def cno(c, k):
            return Count(c, K, k)

        def passed(eng):
            eng.sem_inc(step_done[eng], 1)

        def credit(eng, *signals):
            for s in signals:
                eng.sem_inc(s.h, CREDIT)

        @block.sync
        def _(sp):
            sp.wait_ge(init_dve, 1)
            for dst, src in ((ident[:], t_in["c_ident"]), (spread, t_in["c_spread"]), (gather8[:], t_in["c_gather8"]),
                             (mean192[:], t_in["c_mean192"]), (mean3[:], t_in["c_mean3"]), (order[:], t_in["c_order"])):
                sp.dma_start(dst, src).then_inc(const_in, 16)

            for li, spec, g0, tab in per_layer():
                src_x = t_in["x"] if li == 0 else stream[li - 1]
                dst_x = out if li == len(layers) - 1 else stream[li]
                nm = spec["name"] + "_"
                if li:
                    for i in range(2):
                        sp.wait_ge(xo_st[i].h, xo_st[i].at((0, g0), 0))
                loads = [(w_in[:], t_in[nm + "in_proj_w"]),
                         (cw_rows[0:DM, :], t_in[nm + "conv_w"].unsqueeze(0).broadcast_to([DM, 9 * DI])),
                         (w_xpA[:], t_in[nm + spec["xproj"]][0:P, :]), (w_xpB[:], t_in[nm + spec["xproj"]][P:DI, :]),
                         (w_dt[0:R, :], t_in[nm + spec["dtw"]]), (a_neg[:], t_in[nm + "A_logs"]),
                         (w_outA[:], t_in[nm + "out_proj_w"][0:P, :]), (w_outB[:], t_in[nm + "out_proj_w"][P:DI, :])]
                for col, name, m in ((V_D, "Ds", K), (V_DTB, "dt_projs_bias", K), (V_CB, "conv_b", 1),
                                     (V_G, spec["g"], 1), (V_B, spec["b"], 1)):
                    loads.append((vecA[:, col:col + m], t_in[nm + name][0:P, :]))
                    loads.append((vecB[:, col:col + m], t_in[nm + name][P:DI, :]))
                if tab:
                    loads += [(dir_b[R:R + N, :], t_in[nm + "direction_Bs"]),
                              (coords[0:2, :], t_in["c_coords"]),
                              (pf[0:2, 0:32], t_in[nm + "pf_w1"]), (pf[0:32, 32:33], t_in[nm + "pf_b1"]),
                              (pf[0:32, 36:40], t_in[nm + "pf_w2"]),
                              (pf[:, 40:44], t_in[nm + "pf_b2"].unsqueeze(0).broadcast_to([P, K]))]
                for dst, src in loads:
                    sp.dma_start(dst, src).then_inc(wts_in, 16)
                sp.wait_ge(wts_ok, ready[li])

                with sp.Fori(0, B) as b:
                    gb, tb, nb = (b, g0), (b, 0), (b, g0 - B * sum(is_tab[:li]))
                    if li:
                        for i in range(2):
                            sp.wait_ge(xo_st[i].h, xo_st[i].at(gb, 0))
                    passed(sp)
                    sp.dma_start(x_in[0:DM, :], src_x[b]).then_inc(x_ld.h, 16)
                    if tab:
                        sp.wait_ge(tk_cp.h, tk_cp.at(tb, BLK // 2))
                        sp.dma_start(xtok_d.rearrange("(n p) d -> p n d", p=P),
                                     tok_x.rearrange("p (n d) -> p n d", d=DI)).then_inc(tk_st.h, 16)
                    for k, kind in enumerate(spec["dirs"]):
                        if kind == "n":
                            a, bb = xcA, xcB
                        else:
                            a, bb = permA[k % 2], permB[k % 2]
                        sp.wait_ge(pm_dve.h, pm_dve.at(gb, k + 1))
                        sp.wait_ge(pm_act.h, pm_act.at(gb, k + 1))
                        sp.dma_start(xs_d[k, 0:P, :], a).then_inc(pre_st[k % 2].h, 16)
                        sp.dma_start(xs_d[k, P:DI, :], bb[0:DB, :]).then_inc(pre_st[k % 2].h, 16)
                        sp.wait_ge(xp_dve.h, xp_dve.at(gb, (k + 1) * NS))
                        sp.dma_start(xd_d[k], xdt[k % 2][0:XD, :]).then_inc(pre_st[k % 2].h, 16)
                    for i in range(2):
                        sp.wait_ge(pre_st[i].h, pre_st[i].at(gb, 96))
                        passed(sp)

                    ld = ld_mix if mixed[li] else ld_all

                    def load(c, k):
                        par = k % 2
                        sp.wait_ge(z_pe.h, z_pe.at(gb, cno(c, k) * 2))
                        passed(sp)
                        sp.wait_ge(ev.h, ev.at(gb, (cno(c, k) - 1) * 2))
                        passed(sp)
                        sp.wait_ge(pr.h, pr.at(gb, (cno(c, k) - 1) * UN))
                        passed(sp)
                        cols = bass.ds(c * CH, CH)
                        sp.dma_start(rank[0:R, :], xd_d[k, 0:R, cols]).then_inc(ld_r.h, 16)
                        sp.dma_start(xsA[par], xs_d[k, 0:P, cols]).then_inc(ld[par].h, 16)
                        sp.dma_start(xsB[par][0:DB, :], xs_d[k, P:DI, cols]).then_inc(ld[par].h, 16)
                        for dst, row in ((bt[par], R), (ct[par], R + N)):
                            if mixed[li]:
                                for m in range(K):
                                    src = xd_d[m, row:row + N, cols].unsqueeze(1).broadcast_to([N, G8 // K, CH])
                                    sp.dma_start(dst[m:P:K, :], src).then_inc(ld[par].h, 16)
                            else:
                                src = xd_d[k, row:row + N, cols].unsqueeze(1).broadcast_to([N, G8, CH])
                                sp.dma_start(dst, src).then_inc(ld[par].h, 16)

                    def body(c, k, last):
                        if not last:
                            load(*nxt(c, k))
                        cols = bass.ds(c * CH, CH)
                        sp.wait_ge(ev.h, ev.at(gb, cno(c, k) * 2 + 1))
                        passed(sp)
                        sp.dma_start(y_d[k, 0:P, cols], yoA).then_inc(stA.h, 16)
                        sp.wait_ge(ev.h, ev.at(gb, cno(c, k) * 2 + 2))
                        passed(sp)
                        sp.dma_start(y_d[k, P:DI, cols], yoB[0:DB, :]).then_inc(stB.h, 16)

                    load(0, 0)
                    chunks(sp, body)

                    sp.wait_ge(stA.h, stA.at(gb, CHK * 16))
                    passed(sp)
                    sp.wait_ge(stB.h, stB.at(gb, CHK * 16))
                    passed(sp)
                    sp.wait_ge(ca.h, ca.at(gb, CHK * UN))
                    if not tab:
                        for k in range(K):
                            sp.dma_start(yA[k], y_d[k, 0:P, :]).then_inc(y_ld[0].h, 16)
                        sp.dma_start(yB[0][0:DB, :], y_d[0, P:DI, :]).then_inc(y_ld[1].h, 16)
                        sp.wait_ge(cb.h, cb.at(nb, 3))
                        for k in range(1, K):
                            sp.dma_start(yB[k][0:DB, :], y_d[k, P:DI, :]).then_inc(y_ld[1].h, 16)
                    else:
                        for k in range(K):
                            if k >= 2:
                                sp.wait_ge(yt_pe.h, yt_pe.at(tb, (k - 1) * BLK // 2))
                            sp.dma_start(yin[k % 2][0], y_d[k, 0:P, :]).then_inc(yt_ld[k % 2].h, 16)
                            sp.dma_start(yin[k % 2][1][0:DB, :], y_d[k, P:DI, :]).then_inc(yt_ld[k % 2].h, 16)
                        for i in range(2):
                            sp.wait_ge(ys_st[i].h, ys_st[i].at(tb, K // 2 * BLK * 16))
                        for k in range(K):
                            sp.dma_start(ytok[k].rearrange("p (n d) -> p n d", d=DI),
                                         ytok_d[k].rearrange("(n p) d -> p n d", p=P)).then_inc(yr_ld.h, 16)
                    for s in range(NS + 1):
                        if s < NS:
                            if s == 0:
                                sp.wait_ge(zz_act.h, zz_act.at(gb, 1))
                            if s >= 2:
                                sp.wait_ge(xo.h, xo.at(gb, s - 1))
                            passed(sp)
                            sp.dma_start(xres[s % 2][0:DM, :], src_x[b][:, s * SL:(s + 1) * SL]).then_inc(xr_ld[s % 2].h, 16)
                        if s >= 1:
                            sp.wait_ge(xo.h, xo.at(gb, s))
                            passed(sp)
                            sp.dma_start(dst_x[b][:, (s - 1) * SL:s * SL], xout[(s - 1) % 2][0:DM, :]).then_inc(xo_st[(s - 1) % 2].h, 16)
            for i in range(2):
                sp.wait_ge(xo_st[i].h, xo_st[i].at((0, len(layers) * B), 0))

        @block.tensor
        def _(pe):
            credit(pe, gn_pe, cv_pe, xp_pe, dt_f, du_f, yq, z_pe, zz_pe, mu_pe, va_pe, op_pe,
                   tk_pe, ga_pe, gb_pe, yt_pe, yb_pe)
            pe.wait_ge(const_ok, 2)
            for li, spec, g0, tab in per_layer():
                if tab:
                    pe.wait_ge(wts_in, 16 * counts[li])
                    for i in range(K * NS):
                        if i >= 2:
                            pe.wait_ge(setup_act, i - 1)
                        pe.matmul(bank(i % 2, 32), pf[0:2, 0:32], coords[0:2, i * SL:(i + 1) * SL],
                                  start=True, stop=True).then_inc(setup_pe, 1)
                        pe.wait_ge(setup_act, i + 1)
                        for q in range(4):
                            blk = 4 * i + q
                            mm = pe.matmul(ps[:, 2, 4 * blk:4 * blk + 4], hid[i % 2][0:32, q * P:(q + 1) * P],
                                           pf[0:32, 36:40], start=True, stop=True)
                        mm.then_inc(setup_pe, 1)
                pe.wait_ge(wts_ok, ready[li])
                with pe.Fori(0, B) as b:
                    gb, tb, nb = (b, g0), (b, 0), (b, g0 - B * sum(is_tab[:li]))
                    for i in range(2):
                        pe.wait_ge(gn_dve.h, gn_dve.at(gb, (9, 12)[i]))
                        pe.matmul(ps[0:DM, i, 0:1], mean3[:], gn_v[:, 3 * i:3 * i + 1], start=True, stop=True).then_inc(gn_pe.h, 1)
                    pe.wait_ge(gn_dve.h, gn_dve.at(gb, 13))
                    for i in range(2 * NS):
                        s, half = divmod(i, 2)
                        if i >= 8:
                            pe.wait_ge(cv_act.h, cv_act.at(gb, i - 7))
                        d0, m = (0, P) if half == 0 else (P, DB)
                        rows = SL // WW
                        for tap in range(9):
                            dy, dx = divmod(tap, 3)
                            mm = pe.matmul(bank(i % 8, m), w_conv[:, tap * DI + d0:tap * DI + d0 + m],
                                           xn_img[:, s * rows + dy:s * rows + dy + rows, dx:dx + WW],
                                           start=tap == 0, stop=tap == 8)
                        mm.then_inc(cv_pe.h, 1)
                    pe.wait_ge(cv_act.h, cv_act.at(gb, 2 * NS))
                    if tab:
                        for i in range(BLK // 2):
                            if i >= 4:
                                pe.wait_ge(tk_cp.h, tk_cp.at(tb, i - 3))
                            for q in range(2):
                                blk = 2 * i + q
                                pe.transpose(ps[:, i % 4, q * DI:q * DI + P], xcA[:, blk * P:(blk + 1) * P], ident[:])
                                mm = pe.transpose(ps[:, i % 4, q * DI + P:(q + 1) * DI], xcB[0:DB, blk * P:(blk + 1) * P],
                                                  ident[0:DB, 0:DB])
                            mm.then_inc(tk_pe.h, 1)
                    for k, kind in enumerate(spec["dirs"]):
                        if tab:
                            pe.wait_ge(tg.h, tg.at(tb, (k + 1) * BLK * 16))
                            if k == 0:
                                pe.wait_ge(tk_cp.h, tk_cp.at(tb, BLK // 2))
                            for m in range(NS):
                                i = k * NS + m
                                if m >= 2:
                                    pe.wait_ge(pm_cpA.h, pm_cpA.at(tb, i - 1))
                                    pe.wait_ge(pm_cpB.h, pm_cpB.at(tb, i - 1))
                                elif k:
                                    pe.wait_ge(pm_dve.h, pm_dve.at(gb, k))
                                    pe.wait_ge(pm_act.h, pm_act.at(gb, k))
                                for q in range(4):
                                    blk = 4 * m + q
                                    mm = pe.transpose(ps[:, m % 2, q * P:(q + 1) * P], tok_g[:, blk * DI:blk * DI + P], ident[:])
                                mm.then_inc(ga_pe.h, 1)
                                passed(pe)
                                for q in range(4):
                                    blk = 4 * m + q
                                    mm = pe.transpose(ps[0:DB, 2 + m % 2, q * P:(q + 1) * P],
                                                      tok_g[:, blk * DI + P:(blk + 1) * DI], ident[:])
                                mm.then_inc(gb_pe.h, 1)
                        a, bb = (xcA, xcB) if kind == "n" else (permA[k % 2], permB[k % 2])
                        pe.wait_ge(pm_dve.h, pm_dve.at(gb, k + 1))
                        pe.wait_ge(pm_act.h, pm_act.at(gb, k + 1))
                        for s in range(NS):
                            i = k * NS + s
                            if i >= 4:
                                pe.wait_ge(xp_dve.h, xp_dve.at(gb, i - 3))
                            o = bank(4 + i % 4, XD)
                            pe.matmul(o, w_xpA[:, k * XD:(k + 1) * XD], a[:, s * SL:(s + 1) * SL], start=True, stop=False)
                            pe.matmul(o, w_xpB[:, k * XD:(k + 1) * XD], bb[0:DB, s * SL:(s + 1) * SL],
                                      start=False, stop=True).then_inc(xp_pe.h, 1)
                    pe.wait_ge(xp_dve.h, xp_dve.at(gb, K * NS))

                    def z(c, k, half, spread_so_far):
                        if half == 0:
                            pe.wait_ge(ld_r.h, ld_r.at(gb, (cno(c, k) + 1) * 16))
                        d0, m = (0, P) if half == 0 else (P, DB)
                        pe.wait_ge(ex.h, ex.at(gb, spread_so_far))
                        for h in range(2):
                            mm = pe.matmul(ps_dt[0:m, h * SL:(h + 1) * SL], w_dt[:, k * DI + d0:k * DI + d0 + m],
                                           rank[:, h * SL:(h + 1) * SL], start=True, stop=True)
                        mm.then_inc(z_pe.h, 1)

                    z_at = (6, 12)

                    def spread_rows(dst, tile, par, group, part):
                        for h in range(2):
                            for j, src in enumerate((hi[tile][par], lo[tile][par])):
                                v = (group * 4 + part) * P
                                mm = pe.matmul(dst[:, h * SL:(h + 1) * SL], spread_r[:, v:v + P],
                                               src[:, h * SL:(h + 1) * SL], start=j == 0, stop=j == 1)
                        return mm

                    def unit(c, k, t, z_before=None):
                        first, rg, part = unit_place(t)
                        u = uno(c, k, t)
                        if t == 0:
                            pe.wait_ge(lo_ok.h, lo_ok.at(gb, cno(c, k) * 3 + 2))
                        if t == UA:
                            pe.wait_ge(lo_ok.h, lo_ok.at(gb, cno(c, k) * 3 + 3))
                        for what in ("dt", "du") if z_before is None else ("du", "dt"):
                            if what == "dt":
                                pe.wait_ge(ex.h, ex.at(gb, u))
                                if z_before is not None:
                                    pe.wait_ge(z_act.h, z_act.at(gb, z_before))
                                spread_rows(ps_dt, "dtA" if first else "mixB", k % 2, rg, part).then_inc(dt_f.h, 1)
                            else:
                                pe.wait_ge(sc.h, sc.at(gb, u - 1))
                                spread_rows(ps_du[t % 2], "duA" if first else "mixB", k % 2,
                                            rg if first else 2 + rg, part).then_inc(du_f.h, 1)

                    def quad(c, k, m):
                        pe.wait_ge(pr.h, pr.at(gb, uno(c, k, 4 * m + 4)))
                        if m == 0:
                            pe.wait_ge(ev.h, ev.at(gb, cno(c, k) * 2))
                        if m == 4:
                            pe.wait_ge(ev.h, ev.at(gb, cno(c, k) * 2 + 1))
                        for h in range(2):
                            for t in range(4 * m, 4 * m + 4):
                                _, rg, part = unit_place(t)
                                mm = pe.matmul(ps_y[32 * rg:32 * rg + 32, h * SL:(h + 1) * SL],
                                               gather8[:, part * 32:(part + 1) * 32],
                                               state[t % RH][:, h * SL:(h + 1) * SL], start=part == 0, stop=part == 3)
                        mm.then_inc(yq.h, 1)

                    def body(c, k, last):
                        for t in range(LEAD, UN if last else UN + LEAD):
                            if t < UN:
                                z_before = None
                                if not last and t - 1 in z_at:
                                    z_before = cno(*nxt(c, k)) * 2 + z_at.index(t - 1) + 1
                                unit(c, k, t, z_before)
                            else:
                                unit(*nxt(c, k), t - UN)
                            if not last and t in z_at:
                                z(*nxt(c, k), z_at.index(t), uno(c, k, t + 1))
                            if t >= 7 and t % 4 == 3:
                                quad(c, k, t // 4 - 1)
                        if last:
                            quad(c, k, 5)

                    for half in range(2):
                        z(0, 0, half, 0)
                        pe.wait_ge(z_act.h, z_act.at(gb, half + 1))
                    for t in range(LEAD):
                        unit(0, 0, t)
                    chunks(pe, body)

                    if not tab:
                        pe.wait_ge(cb.h, cb.at(nb, 6))
                    else:
                        for i in range(K * BLK // 2):
                            k, m = divmod(i, BLK // 2)
                            if i == 0:
                                pe.wait_ge(ev.h, ev.at(gb, CHK * 2))
                            if m == 0:
                                pe.wait_ge(yt_ld[k % 2].h, yt_ld[k % 2].at(tb, (k // 2 + 1) * 32))
                            if i >= 4:
                                pe.wait_ge(yt_act.h, yt_act.at(tb, i - 3))
                            for q in range(2):
                                blk = 2 * m + q
                                pe.transpose(ps[:, i % 4, q * DI:q * DI + P], yin[k % 2][0][:, blk * P:(blk + 1) * P], ident[:])
                                mm = pe.transpose(ps[:, i % 4, q * DI + P:(q + 1) * DI],
                                                  yin[k % 2][1][0:DB, blk * P:(blk + 1) * P], ident[0:DB, 0:DB])
                            mm.then_inc(yt_pe.h, 1)
                        pe.wait_ge(yt_act.h, yt_act.at(tb, K * BLK // 2))
                        pe.wait_ge(yr_ad.h, yr_ad.at(tb, 3))
                        for i in range(2 * NS):
                            m, half = divmod(i, 2)
                            if i >= 4:
                                pe.wait_ge(yb_cp.h, yb_cp.at(tb, i - 3))
                            passed(pe)
                            for q in range(4):
                                blk = 4 * m + q
                                c0, w = (0, P) if half == 0 else (P, DB)
                                mm = pe.transpose(ps[0:w, i % 4, q * P:(q + 1) * P],
                                                  ytok[0][:, blk * DI + c0:blk * DI + c0 + w], ident[:])
                            mm.then_inc(yb_pe.h, 1)
                        pe.wait_ge(yb_cp.h, yb_cp.at(tb, 2 * NS))
                    for i in range(2 * NS):
                        s, half = divmod(i, 2)
                        if i >= 2:
                            pe.wait_ge(zz_act.h, zz_act.at(gb, i - 1))
                        d0, m = (DI, P) if half == 0 else (DI + P, DB)
                        rows = SL // WW
                        pe.matmul(bank(6 + i % 2, m), w_in[:, d0:d0 + m],
                                  xn_img[:, s * rows + 1:s * rows + 1 + rows, 1:1 + WW],
                                  start=True, stop=True).then_inc(zz_pe.h, 1)
                    for s in range(NS + 3):
                        if s < NS:
                            if s >= 2:
                                pe.wait_ge(yc.h, yc.at(gb, s - 1))
                            cols = slice(s * SL, (s + 1) * SL)
                            pe.matmul(bank(s % 2), mean192[:], post_y(tab)[0][:, cols], start=True, stop=False)
                            pe.matmul(bank(s % 2), mean192[0:DB, :], post_y(tab)[1][0:DB, cols],
                                      start=False, stop=True).then_inc(mu_pe.h, 1)
                        v = s - 1
                        if 0 <= v < NS:
                            pe.wait_ge(sq_act.h, sq_act.at(gb, v + 1))
                            if v >= 2:
                                pe.wait_ge(ln_act.h, ln_act.at(gb, v - 1))
                            pe.matmul(bank(2 + v % 2), mean192[:], sq[v % 2][:, 0:SL], start=True, stop=False)
                            pe.matmul(bank(2 + v % 2), mean192[0:DB, :], sq[v % 2][0:DB, SL:2 * SL],
                                      start=False, stop=True).then_inc(va_pe.h, 1)
                        o = s - 3
                        if 0 <= o < NS:
                            pe.wait_ge(gt.h, gt.at(gb, o + 1))
                            if o >= 2:
                                pe.wait_ge(xo.h, xo.at(gb, o - 1))
                            cols = slice(o * SL, (o + 1) * SL)
                            pe.matmul(bank(4 + o % 2, DM), w_outA[:], post_y(tab)[0][:, cols], start=True, stop=False)
                            pe.matmul(bank(4 + o % 2, DM), w_outB[:], post_y(tab)[1][0:DB, cols],
                                      start=False, stop=True).then_inc(op_pe.h, 1)
                    pe.wait_ge(xo.h, xo.at(gb, NS))

        @block.scalar
        def _(act):
            credit(act, gn_act, cv_act, pm_act, pm_cpB, ex, ca, z_act, sp_a, sp_e, sp_w, sp_l, hi_ok,
                   zz_act, sq_act, ln_act, rs_act, af, yt_act)
            for li, spec, g0, tab in per_layer():
                act.wait_ge(wts_in, 16 * counts[li])
                act.activation(a_neg[:], a_neg[:], ACT.Exp).then_inc(setup_exp, 1)
                if tab:
                    for i in range(K * NS):
                        act.wait_ge(setup_pe, 2 * i + 1)
                        if i >= 2:
                            act.wait_ge(setup_pe, 2 * (i - 1))
                        act.activation(hid[i % 2][0:32, :], bank(i % 2, 32), ACT.Gelu, bias=pf[0:32, 32:33]).then_inc(setup_act, 1)
                    act.wait_ge(setup_dve, 3)
                    act.activation(logit[1], logit[1], ACT.Exp).then_inc(setup_exp, 1)
                act.wait_ge(wts_ok, ready[li])
                with act.Fori(0, B) as b:
                    gb, tb, nb = (b, g0), (b, 0), (b, g0 - B * sum(is_tab[:li]))
                    act.preload_act_table_set("natural_log_exp_and_others")
                    act.wait_ge(gn_pe.h, gn_pe.at(gb, 2))
                    act.activation(gn_v[:, 6:7], ps[0:DM, 1, 0:1], ACT.Ln, bias=gn_v[:, 8:9]).then_inc(gn_act.h, 1)
                    act.wait_ge(gn_act.h, gn_act.at(gb, 1))
                    act.activation(gn_v[:, 7:8], gn_v[:, 6:7], ACT.Exp, scale=-0.5).then_inc(gn_act.h, 1)
                    for i in range(2 * NS):
                        s, half = divmod(i, 2)
                        act.wait_ge(cv_pe.h, cv_pe.at(gb, i + 1))
                        m, dst, vec = (P, xcA, vecA) if half == 0 else (DB, xcB, vecB)
                        act.activation(dst[0:m, s * SL:(s + 1) * SL], bank(i % 8, m), ACT.Silu,
                                       bias=vec[:, V_CB:V_CB + 1]).then_inc(cv_act.h, 1)
                    act.wait_ge(cv_act.h, cv_act.at(gb, 2 * NS))
                    for k, kind in enumerate(spec["dirs"]):
                        if k >= 2:
                            act.wait_ge(pre_st[k % 2].h, pre_st[k % 2].at(gb, 48 * (k // 2)))
                        if kind == "g":
                            for m in range(NS):
                                act.wait_ge(gb_pe.h, gb_pe.at(tb, k * NS + m + 1))
                                act.activation(permB[k % 2][0:DB, m * SL:(m + 1) * SL], bank(2 + m % 2, DB),
                                               ACT.Copy).then_inc(pm_cpB.h, 1)
                            act.wait_ge(pm_cpB.h, pm_cpB.at(tb, (k + 1) * NS))
                            act.sem_inc(pm_act.h, 1)
                        elif kind == "n":
                            act.sem_inc(pm_act.h, 1)
                        else:
                            act.activation(permB[k % 2][0:DB, :].rearrange("p (a b) -> p a b", b=WW),
                                           ordered(xcB[0:DB, :], kind), ACT.Copy).then_inc(pm_act.h, 1)

                    act.preload_act_table_set("natural_log_exp_and_others")

                    def decays(c, k, t):
                        u = uno(c, k, t)
                        act.wait_ge(dt_f.h, dt_f.at(gb, u + 1))
                        act.wait_ge(sc.h, sc.at(gb, u - RDA + 1))
                        act.activation(decay[(t) % RDA], ps_dt, ACT.Exp,
                                       scale=a_neg[:, k * UN + t:k * UN + t + 1]).then_inc(ex.h, 1)

                    def keep(c, k, t):
                        act.wait_ge(sc.h, sc.at(gb, uno(c, k, t) + 1))
                        act.activation(carry[:, k * UN + t:k * UN + t + 1], state[t % RH][:, CH - 1:CH],
                                       ACT.Copy).then_inc(ca.h, 1)

                    def soft(c, k, half, step):
                        m, vec = (P, vecA) if half == 0 else (DB, vecB)
                        n = cno(c, k) * 2 + half
                        bias = vec[:, V_DTB + k:V_DTB + k + 1]
                        if step == 0:
                            act.wait_ge(z_pe.h, z_pe.at(gb, n + 1))
                            act.wait_ge(sp_r.h, sp_r.at(gb, n))
                            act.wait_ge(sp_l.h, sp_l.at(gb, n))
                            act.activation(wz[0:m, :], ps_dt[0:m, :], ACT.Identity, bias=bias).then_inc(z_act.h, 1)
                        elif step == 1:
                            act.wait_ge(z_act.h, z_act.at(gb, n + 1))
                            act.wait_ge(lo_ok.h, lo_ok.at(gb, cno(c, k) * 3))
                            act.activation(rz[half][0:m, :], wz[0:m, :], ACT.Relu)
                            act.activation(az[half][0:m, :], wz[0:m, :], ACT.Abs).then_inc(sp_a.h, 1)
                        elif step == 2:
                            act.wait_ge(sp_a.h, sp_a.at(gb, n + 1))
                            act.activation(az[half][0:m, :], az[half][0:m, :], ACT.Exp, scale=-1.0).then_inc(sp_e.h, 1)
                        elif step == 3:
                            act.wait_ge(sp_e.h, sp_e.at(gb, n + 1))
                            act.activation(wz[0:m, :], az[half][0:m, :], ACT.Identity, bias=1.0).then_inc(sp_w.h, 1)
                        else:
                            act.wait_ge(sp_w.h, sp_w.at(gb, n + 1))
                            act.wait_ge(dt_ok.h, dt_ok.at(gb, n))
                            act.activation(lz[0:m, :], wz[0:m, :], ACT.Ln).then_inc(sp_l.h, 1)

                    def split(c, k, i):
                        s = (dt_ok, du_ok, du_ok)[i]
                        act.wait_ge(s.h, s.at(gb, cno(c, k) * 2 + (1, 1, 2)[i]))
                        act.activation(hi[("dtA", "duA", "mixB")[i]][k % 2], (rz[0], az[0], rz[1])[i], ACT.Copy).then_inc(hi_ok.h, 1)

                    steps = {6: (soft, 0, 0), 7: (soft, 0, 1), 8: (soft, 0, 2), 9: (soft, 0, 3), 10: (soft, 0, 4),
                             12: (soft, 1, 0), 13: (soft, 1, 1), 14: (soft, 1, 2), 15: (soft, 1, 3), 19: (soft, 1, 4),
                             20: (split, 0), 21: (split, 1), 26: (split, 2)}

                    def body(c, k, last):
                        for t in range(LEAD, UN + (2 if last else LEAD)):
                            if t < UN:
                                decays(c, k, t)
                            elif not last:
                                decays(*nxt(c, k), t - UN)
                            if t - 2 < UN:
                                keep(c, k, t - 2)
                            else:
                                keep(*nxt(c, k), t - 2 - UN)
                            if not last and t in steps:
                                fn, *args = steps[t]
                                fn(*nxt(c, k), *args)

                    act.wait_ge(xp_dve.h, xp_dve.at(gb, K * NS))
                    for i in range(2):
                        act.wait_ge(pre_st[i].h, pre_st[i].at(gb, 96))
                    for half in range(2):
                        for step in range(5):
                            soft(0, 0, half, step)
                        for i in ((0, 1), (2,))[half]:
                            split(0, 0, i)
                    for t in range(LEAD):
                        decays(0, 0, t)
                        if t >= 2:
                            keep(0, 0, t - 2)
                    chunks(act, body)

                    if tab:
                        for i in range(K * BLK // 2):
                            k, m = divmod(i, BLK // 2)
                            if m == 0 and k >= 2:
                                act.wait_ge(ys_st[k % 2].h, ys_st[k % 2].at(tb, k // 2 * BLK * 16))
                            act.wait_ge(yt_pe.h, yt_pe.at(tb, i + 1))
                            for q in range(2):
                                blk = 2 * m + q
                                ins = act.activation(tok_o[k % 2][:, blk * DI:(blk + 1) * DI], ps[:, i % 4, q * DI:(q + 1) * DI],
                                                     ACT.Copy, scale=w_pos[:, k * BLK + blk:k * BLK + blk + 1])
                            ins.then_inc(yt_act.h, 1)
                        act.wait_ge(yb_cp.h, yb_cp.at(tb, 2 * NS))
                    else:
                        act.wait_ge(cb.h, cb.at(nb, 6))
                    for i in range(2 * NS):
                        s, half = divmod(i, 2)
                        act.wait_ge(zz_pe.h, zz_pe.at(gb, i + 1))
                        m, dst = (P, zsA) if half == 0 else (DB, zsB)
                        act.activation(dst[0:m, s * SL:(s + 1) * SL], bank(6 + i % 2, m), ACT.Silu).then_inc(zz_act.h, 1)
                    act.preload_act_table_set("natural_log_exp_and_others")
                    for s in range(NS + 2):
                        if s < NS:
                            act.wait_ge(yc.h, yc.at(gb, s + 1))
                            if s >= 2:
                                act.wait_ge(va_pe.h, va_pe.at(gb, s - 1))
                            cols = slice(s * SL, (s + 1) * SL)
                            act.activation(sq[s % 2][:, 0:SL], post_y(tab)[0][:, cols], ACT.Square)
                            act.activation(sq[s % 2][0:DB, SL:2 * SL], post_y(tab)[1][0:DB, cols], ACT.Square).then_inc(sq_act.h, 1)
                        v = s - 1
                        if 0 <= v < NS:
                            act.wait_ge(va_pe.h, va_pe.at(gb, v + 1))
                            if v >= 3:
                                act.wait_ge(yn.h, yn.at(gb, v - 2))
                            act.activation(rs[v % 3], bank(2 + v % 2), ACT.Ln, bias=ln_eps(li)).then_inc(ln_act.h, 1)
                            act.wait_ge(ln_act.h, ln_act.at(gb, v + 1))
                            act.activation(rs[v % 3], rs[v % 3], ACT.Exp, scale=-0.5).then_inc(rs_act.h, 1)
                        a = s - 2
                        if 0 <= a < NS:
                            act.wait_ge(yn.h, yn.at(gb, a + 1))
                            cols = slice(a * SL, (a + 1) * SL)
                            for m, yy, vec in ((P, post_y(tab)[0], vecA), (DB, post_y(tab)[1], vecB)):
                                ins = act.activation(yy[0:m, cols], yy[0:m, cols], ACT.Identity,
                                                     scale=vec[:, V_G:V_G + 1], bias=vec[:, V_B:V_B + 1])
                            ins.then_inc(af.h, 1)

        @block.vector
        def _(dve):
            credit(dve, gn_dve, pm_dve, pm_cpA, xp_dve, dbu, sc, ev, sp_r, cz, cb, yc, yn, xo, yr_ad, yb_cp, tk_cp)
            dve.memset(vecA[:, 11:12], 1e-6)
            dve.memset(vecA[:, 12:13], 1e-5)
            dve.memset(dir_b[:], 0.0)
            dve.memset(w_dt[:], 0.0)
            dve.memset(rank, 0.0)
            dve.memset(gn_v[:, 8:9], 1e-5).then_inc(init_dve, 1)
            dve.wait_ge(const_in, 96)
            dve.tensor_copy(spread_r[:], spread).then_inc(const_ok, 1)
            dve.wait_ge(init_dve, 1)
            for li, spec, g0, tab in per_layer():
                dve.wait_ge(wts_in, 16 * counts[li])
                dve.tensor_tensor(w_conv[:].rearrange("p (t d) -> p t d", d=DI),
                                  cw_rows[0:DM, :].rearrange("p (t d) -> p t d", d=DI),
                                  w_in[:, 0:DI].unsqueeze(1).broadcast_to([DM, 9, DI]), ALU.mult).then_inc(wts_ok, 1)
                exps = li + 1 + sum(is_tab[:li])
                dve.wait_ge(setup_exp, exps)
                dve.tensor_scalar(a_neg[:], a_neg[:], -1.0, None, ALU.mult).then_inc(wts_ok, 1)
                if tab:
                    lg = [v.rearrange("p (t k) -> p t k", k=K) for v in logit]
                    dve.wait_ge(setup_pe, 2 * K * NS)
                    dve.tensor_tensor(lg[0], ps[:, 2, :].rearrange("p (t k) -> p t k", k=K),
                                      pf[:, 40:44].unsqueeze(1).broadcast_to([P, P, K]), ALU.add).then_inc(setup_dve, 1)
                    dve.wait_ge(setup_dve, 1)
                    dve.tensor_reduce(red[0], lg[0], AX_X, ALU.max).then_inc(setup_dve, 1)
                    dve.wait_ge(setup_dve, 2)
                    dve.tensor_tensor(lg[1], lg[0], red[0].unsqueeze(2).broadcast_to([P, P, K]), ALU.subtract).then_inc(setup_dve, 1)
                    dve.wait_ge(setup_exp, exps + 1)
                    dve.tensor_reduce(red[1], lg[1], AX_X, ALU.add).then_inc(setup_dve, 1)
                    dve.wait_ge(setup_dve, 4)
                    dve.reciprocal(red[2], red[1]).then_inc(setup_dve, 1)
                    dve.wait_ge(setup_dve, 5)
                    for k in range(K):
                        dve.tensor_tensor(w_pos[:, k * BLK:(k + 1) * BLK], lg[1][:, k * BLK:(k + 1) * BLK, k],
                                          red[2][:, k * BLK:(k + 1) * BLK], ALU.mult).then_inc(wts_ok, 1)
                with dve.Fori(0, B) as b:
                    gb, tb, nb = (b, g0), (b, 0), (b, g0 - B * sum(is_tab[:li]))
                    dve.wait_ge(x_ld.h, x_ld.at(gb, 16))
                    for s in range(NS):
                        dve.bn_stats(gn_s[:, 6 * s:6 * s + 6], x_in[0:DM, s * SL:(s + 1) * SL]).then_inc(gn_dve.h, 1)
                    dve.wait_ge(gn_dve.h, gn_dve.at(gb, 8))
                    passed(dve)
                    dve.bn_aggr(gn_v[:, 0:2], gn_s[:]).then_inc(gn_dve.h, 1)
                    dve.wait_ge(gn_dve.h, gn_dve.at(gb, 9))
                    dve.wait_ge(gn_pe.h, gn_pe.at(gb, 1))
                    dve.tensor_tensor(gn_v[:, 2:3], gn_v[:, 0:1], ps[0:DM, 0, 0:1], ALU.subtract).then_inc(gn_dve.h, 1)
                    dve.tensor_copy(gn_v[:, 4:5], ps[0:DM, 0, 0:1]).then_inc(gn_dve.h, 1)
                    dve.wait_ge(gn_dve.h, gn_dve.at(gb, 11))
                    dve.scalar_tensor_tensor(gn_v[:, 3:4], gn_v[:, 2:3], gn_v[:, 2:3], gn_v[:, 1:2], ALU.mult, ALU.add).then_inc(gn_dve.h, 1)
                    dve.wait_ge(gn_act.h, gn_act.at(gb, 2))
                    dve.wait_ge(const_ok, 2)
                    dve.tensor_scalar(xn_img[:, 1:1 + HH, 1:1 + WW], x_in[0:DM, :].rearrange("p (h w) -> p h w", w=WW),
                                      gn_v[:, 4:5], gn_v[:, 7:8], ALU.subtract, ALU.mult).then_inc(gn_dve.h, 1)
                    dve.wait_ge(cv_act.h, cv_act.at(gb, 2 * NS))
                    if tab:
                        for i in range(BLK // 2):
                            dve.wait_ge(tk_pe.h, tk_pe.at(tb, i + 1))
                            dve.tensor_copy(tok_x[:, 2 * i * DI:(2 * i + 2) * DI], ps[:, i % 4, 0:2 * DI]).then_inc(tk_cp.h, 1)

                    def in_order(k):
                        kind = spec["dirs"][k]
                        if k >= 2:
                            dve.wait_ge(pre_st[k % 2].h, pre_st[k % 2].at(gb, 48 * (k // 2)))
                        if kind == "g":
                            if k == 1:
                                dve.wait_ge(tk_st.h, tk_st.at(tb, 16))
                            for m in range(NS):
                                dve.wait_ge(ga_pe.h, ga_pe.at(tb, k * NS + m + 1))
                                dve.tensor_copy(permA[k % 2][:, m * SL:(m + 1) * SL], bank(m % 2)).then_inc(pm_cpA.h, 1)
                            dve.wait_ge(pm_cpA.h, pm_cpA.at(tb, (k + 1) * NS))
                            dve.sem_inc(pm_dve.h, 1)
                        elif kind == "n":
                            dve.sem_inc(pm_dve.h, 1)
                        else:
                            dve.tensor_copy(permA[k % 2].rearrange("p (a b) -> p a b", b=WW), ordered(xcA, kind)).then_inc(pm_dve.h, 1)

                    def copy_xproj(k):
                        for s in range(NS):
                            dve.wait_ge(xp_pe.h, xp_pe.at(gb, k * NS + s + 1))
                            o = xdt[k % 2][0:XD, s * SL:(s + 1) * SL]
                            if tab:
                                ins = dve.tensor_scalar(o, bank(4 + s % 4, XD), dir_b[:, k:k + 1], None, ALU.add)
                            else:
                                ins = dve.tensor_copy(o, bank(4 + s % 4, XD))
                            ins.then_inc(xp_dve.h, 1)

                    in_order(0)
                    for k in range(K):
                        if k + 1 < K and not tab:
                            in_order(k + 1)
                        copy_xproj(k)
                        if k + 1 < K and tab:
                            in_order(k + 1)

                    dve.wait_ge(ca.h, ca.at(gb, 0))
                    dve.memset(carry[:], 0.0).then_inc(cz.h, 1)
                    dve.wait_ge(cz.h, cz.at(gb, 1))

                    def unit(c, k, t):
                        u = uno(c, k, t)
                        if t == 0:
                            loaded(dve, li, b, c, k)
                        dve.wait_ge(du_f.h, du_f.at(gb, u + 1))
                        dve.tensor_tensor(ps_du[t % 2], ps_du[t % 2], bt[k % 2], ALU.mult).then_inc(dbu.h, 1)
                        dve.wait_ge(ex.h, ex.at(gb, u + 1))
                        dve.wait_ge(yq.h, yq.at(gb, cno(c, k) * 6 + (t // 4 - 1)))
                        dve.wait_ge(dbu.h, dbu.at(gb, u + 1))
                        col = k * UN + t
                        dve.tensor_tensor_scan(state[t % RH], decay[t % RDA], ps_du[t % 2], carry[:, col:col + 1],
                                               ALU.mult, ALU.add).then_inc(sc.h, 1)

                    def out_y(c, k, half):
                        n = cno(c, k)
                        dve.wait_ge(yq.h, yq.at(gb, n * 6 + (4 if half == 0 else 6)))
                        st = stA if half == 0 else stB
                        dve.wait_ge(st.h, st.at(gb, n * 16))
                        m, x, o, vec = (P, xsA, yoA, vecA) if half == 0 else (DB, xsB, yoB, vecB)
                        dve.scalar_tensor_tensor(o[0:m, :], x[k % 2][0:m, :], vec[:, V_D + k:V_D + k + 1], ps_y[0:m, :],
                                                 ALU.mult, ALU.add).then_inc(ev.h, 1)

                    def rest(c, k, half):
                        n, m = cno(c, k) * 2 + half, (P, DB)[half]
                        dve.wait_ge(sp_w.h, sp_w.at(gb, n + 1))
                        dve.scalar_tensor_tensor(az[half][0:m, :], wz[0:m, :], -1.0, az[half][0:m, :], ALU.add, ALU.subtract).then_inc(sp_r.h, 1)

                    def du_b(c, k):
                        dve.wait_ge(dt_ok.h, dt_ok.at(gb, cno(c, k) * 2 + 2))
                        loaded(dve, li, b, c, k)
                        dve.tensor_tensor(rz[1][DB:P, :], rz[1][0:DB, :], xsB[k % 2][0:DB, :], ALU.mult).then_inc(du_ok.h, 1)

                    def body(c, k, last):
                        for t in range(LEAD, UN if last else UN + LEAD):
                            if t < UN:
                                unit(c, k, t)
                            else:
                                unit(*nxt(c, k), t - UN)
                            if not last:
                                if t == 8:
                                    rest(*nxt(c, k), 0)
                                if t == 14:
                                    rest(*nxt(c, k), 1)
                                if t == 23:
                                    du_b(*nxt(c, k))
                            if t == 22:
                                out_y(c, k, 0)
                        out_y(c, k, 1)

                    rest(0, 0, 0)
                    rest(0, 0, 1)
                    du_b(0, 0)
                    for t in range(LEAD):
                        unit(0, 0, t)
                    chunks(dve, body)

                    if not tab:
                        byk = {kind: k for k, kind in enumerate(spec["dirs"])}
                        for half, (yy, m) in enumerate(((yA, P), (yB, DB))):
                            y = [v[0:m, :] for v in yy]
                            dve.wait_ge(y_ld[half].h, y_ld[half].at(nb, 64))
                            kw, krw, krn = byk["w"], byk["rw"], byk["rn"]
                            dve.tensor_tensor(y[kw], y[kw], y[krw][:, ::-1], ALU.add).then_inc(cb.h, 1)
                            dve.tensor_tensor(y[0], y[0], y[krn][:, ::-1], ALU.add).then_inc(cb.h, 1)
                            dve.wait_ge(cb.h, cb.at(nb, 3 * half + 2))
                            v0 = y[0].rearrange("p (h w) -> p h w", w=WW)
                            dve.tensor_tensor(v0, v0, y[kw].rearrange("p (w h) -> p h w", h=HH), ALU.add).then_inc(cb.h, 1)
                    else:
                        dve.wait_ge(yr_ld.h, yr_ld.at(tb, K * 16))
                        dve.tensor_tensor(ytok[0], ytok[0], ytok[1], ALU.add).then_inc(yr_ad.h, 1)
                        dve.tensor_tensor(ytok[2], ytok[2], ytok[3], ALU.add).then_inc(yr_ad.h, 1)
                        dve.wait_ge(yr_ad.h, yr_ad.at(tb, 2))
                        dve.tensor_tensor(ytok[0], ytok[0], ytok[2], ALU.add).then_inc(yr_ad.h, 1)
                        dve.wait_ge(yr_ad.h, yr_ad.at(tb, 3))
                        for i in range(2 * NS):
                            m, half = divmod(i, 2)
                            w = (P, DB)[half]
                            dve.wait_ge(yb_pe.h, yb_pe.at(tb, i + 1))
                            dve.tensor_copy(post_y(tab)[half][0:w, m * SL:(m + 1) * SL], bank(i % 4, w)).then_inc(yb_cp.h, 1)
                    for s in range(NS + 4):
                        if s < NS:
                            dve.wait_ge(mu_pe.h, mu_pe.at(gb, s + 1))
                            cols = slice(s * SL, (s + 1) * SL)
                            for m, yy in ((P, post_y(tab)[0]), (DB, post_y(tab)[1])):
                                ins = dve.tensor_tensor(yy[0:m, cols], yy[0:m, cols], bank(s % 2, m), ALU.subtract)
                            ins.then_inc(yc.h, 1)
                        v = s - 2
                        if 0 <= v < NS:
                            dve.wait_ge(rs_act.h, rs_act.at(gb, v + 1))
                            cols = slice(v * SL, (v + 1) * SL)
                            for m, yy in ((P, post_y(tab)[0]), (DB, post_y(tab)[1])):
                                ins = dve.tensor_tensor(yy[0:m, cols], yy[0:m, cols], rs[v % 3][0:m, :], ALU.mult)
                            ins.then_inc(yn.h, 1)
                        o = s - 4
                        if 0 <= o < NS:
                            dve.wait_ge(op_pe.h, op_pe.at(gb, o + 1))
                            dve.wait_ge(xr_ld[o % 2].h, xr_ld[o % 2].at(gb, (o // 2 + 1) * 16))
                            dve.wait_ge(xo_st[o % 2].h, xo_st[o % 2].at(gb, o // 2 * 16))
                            dve.tensor_tensor(xout[o % 2][0:DM, :], xres[o % 2][0:DM, :], bank(4 + o % 2, DM), ALU.add).then_inc(xo.h, 1)

        @block.gpsimd
        def _(pool):
            pool.memset(xn[:], 0.0).then_inc(const_ok, 1)
            credit(pool, pr, sp_s, dt_ok, du_ok, lo_ok, gt)
            pool.wait_ge(const_in, 96)
            for li, spec, g0, tab in per_layer():
                pool.wait_ge(wts_ok, ready[li])
                with pool.Fori(0, B) as b:
                    gb, tb, nb = (b, g0), (b, 0), (b, g0 - B * sum(is_tab[:li]))
                    if tab:
                        pool.wait_ge(tk_st.h, tk_st.at(tb, 16))
                        for k in range(K):
                            if k:
                                pool.wait_ge(gb_pe.h, gb_pe.at(tb, k * NS))
                                pool.wait_ge(ga_pe.h, ga_pe.at(tb, k * NS))
                            passed(pool)
                            for blk in range(BLK):
                                pool.indirect_dma_start(
                                    out=tok_g[:, blk * DI:(blk + 1) * DI], out_offset=None, in_=xtok_d,
                                    in_offset=bass.IndirectOffsetOnAxis(ap=order[:, k * BLK + blk:k * BLK + blk + 1], axis=0),
                                ).then_inc(tg.h, 16)

                    def unit(c, k, t):
                        pool.wait_ge(ca.h, ca.at(gb, uno(c, k, t) + 1))
                        pool.tensor_tensor(state[t % RH], state[t % RH], ct[k % 2], ALU.mult).then_inc(pr.h, 1)

                    def soft(c, k, half, step):
                        m, n = (P, DB)[half], cno(c, k) * 2 + half
                        if step == 0:
                            pool.wait_ge(sp_r.h, sp_r.at(gb, n + 1))
                            pool.tensor_tensor(rz[half][0:m, :], rz[half][0:m, :], az[half][0:m, :], ALU.subtract).then_inc(sp_s.h, 1)
                        elif step == 1:
                            pool.wait_ge(sp_l.h, sp_l.at(gb, n + 1))
                            pool.wait_ge(sp_s.h, sp_s.at(gb, n + 1))
                            pool.tensor_tensor(rz[half][0:m, :], rz[half][0:m, :], lz[0:m, :], ALU.add).then_inc(dt_ok.h, 1)
                        else:
                            pool.wait_ge(dt_ok.h, dt_ok.at(gb, n + 1))
                            loaded(pool, li, b, c, k)
                            pool.tensor_tensor(az[half][0:m, :], rz[half][0:m, :], xsA[k % 2], ALU.mult).then_inc(du_ok.h, 1)

                    def split(c, k, i):
                        tile = ("dtA", "duA", "mixB")[i]
                        pool.wait_ge(hi_ok.h, hi_ok.at(gb, cno(c, k) * 3 + i + 1))
                        pool.tensor_tensor(lo[tile][k % 2], (rz[0], az[0], rz[1])[i], hi[tile][k % 2].bitcast(F32),
                                           ALU.subtract).then_inc(lo_ok.h, 1)

                    steps = {8: (soft, 0, 0), 10: (soft, 0, 1), 12: (soft, 0, 2), 14: (soft, 1, 0), 18: (soft, 1, 1),
                             19: (split, 0), 20: (split, 1), 24: (split, 2)}

                    def body(c, k, last):
                        for t in range(LEAD, UN if last else UN + LEAD):
                            if t < UN:
                                unit(c, k, t)
                            else:
                                unit(*nxt(c, k), t - UN)
                            if not last and t in steps:
                                fn, *args = steps[t]
                                fn(*nxt(c, k), *args)

                    for fn, *args in ((soft, 0, 0), (soft, 0, 1), (soft, 0, 2), (split, 0), (split, 1),
                                      (soft, 1, 0), (soft, 1, 1), (split, 2)):
                        fn(0, 0, *args)
                    for t in range(LEAD):
                        unit(0, 0, t)
                    chunks(pool, body)

                    if tab:
                        for k in range(K):
                            pool.wait_ge(yt_act.h, yt_act.at(tb, (k + 1) * BLK // 2))
                            passed(pool)
                            for blk in range(BLK):
                                pool.indirect_dma_start(
                                    out=ytok_d[k], out_offset=bass.IndirectOffsetOnAxis(
                                        ap=order[:, k * BLK + blk:k * BLK + blk + 1], axis=0),
                                    in_=tok_o[k % 2][:, blk * DI:(blk + 1) * DI], in_offset=None,
                                ).then_inc(ys_st[k % 2].h, 16)
                    for s in range(NS):
                        pool.wait_ge(af.h, af.at(gb, s + 1))
                        pool.wait_ge(zz_act.h, zz_act.at(gb, 2 * NS))
                        cols = slice(s * SL, (s + 1) * SL)
                        for m, yy, zz in ((P, post_y(tab)[0], zsA), (DB, post_y(tab)[1], zsB)):
                            ins = pool.tensor_tensor(yy[0:m, cols], yy[0:m, cols], zz[0:m, cols], ALU.mult)
                        ins.then_inc(gt.h, 1)


def scan_orders():
    o1, o2 = [], []
    for s in range(HH + WW - 1):
        ii = range(max(0, s - WW + 1), min(HH, s + 1))
        for o, coords in ((o1, [i * WW + (s - i) for i in ii]),
                          (o2, [i * WW + WW - 1 - (s - i) for i in ii if 0 <= WW - 1 - (s - i) < WW])):
            o.extend(coords[::-1] if s % 2 == 1 else coords)
    yy, xx = np.meshgrid(np.arange(HH), np.arange(WW), indexing="ij")
    dy, dx = yy - HH // 2, xx - WW // 2
    r = np.sqrt(dy ** 2 + dx ** 2)
    th = np.arctan2(dy, dx)
    o3 = np.argsort((r * (L + 1) + (th + np.pi) * 10).flatten())
    o4 = np.argsort((-r * (L + 1) + (th + np.pi) * 10).flatten())
    return np.stack([np.array(o1), np.array(o2), o3, o4])


def constants():
    f = np.float32
    p = np.arange(P)
    spread = np.zeros((P, 4, 4, P), f)
    gather = np.zeros((P, 4, 32), f)
    for q in range(4):
        for d in range(G8):
            for r in range(4):
                spread[32 * r + 8 * q + d, r, q, d::G8] = 1
            gather[np.ix_(p[p % G8 == d], [q], [8 * q + d])] = 1
    c = np.arange(DM)
    mean3 = (c[:, None] // 3 == c[None, :] // 3).astype(f) / f(3)
    idx = scan_orders()
    i = np.arange(HH, dtype=f)
    yy, xx = np.meshgrid((i - f(HH / 2)) / f(HH / 2), (i - f(WW / 2)) / f(WW / 2), indexing="ij")
    r = np.minimum(np.sqrt(yy ** 2 + xx ** 2), f(2.0))
    th = np.arctan2(yy, xx) / f(np.pi)
    coords = np.stack([r.ravel(), th.ravel()]).astype(f)[:, idx.ravel()]
    return {
        "c_ident": np.eye(P, dtype=f), "c_spread": spread.reshape(P, -1), "c_gather8": gather.reshape(P, -1),
        "c_mean192": np.full((P, P), 1 / DI, f), "c_mean3": mean3, "c_coords": coords,
        "c_order": np.ascontiguousarray(idx.reshape(K * BLK, P).T).astype(np.uint32),
    }


def laid_out(name, a):
    a = np.asarray(a)
    tail = name.split("conv_", 1)[-1]
    if name == "x":
        a = a.reshape(a.shape[0], L, DM).transpose(0, 2, 1)
    elif tail in ("in_proj_w", "out_proj_w", "direction_Bs", "pf_w1", "pf_w2"):
        a = a.T
    elif tail == "conv_w":
        a = a.reshape(DI, 9).T.reshape(9 * DI)
    elif tail in ("x_proj_w", "x_proj_weight"):
        a = a.reshape(K * XD, DI).T
    elif tail in ("dt_projs_w", "dt_projs_weight"):
        a = a.reshape(K * DI, R).T
    elif tail == "A_logs":
        a = a.reshape(K, DI, N)
        first = a[:, :P].reshape(K, 4, 4, G8, N).transpose(4, 3, 0, 2, 1).reshape(P, K, UA)
        second = a[:, P:].reshape(K, 2, 4, G8, N).transpose(4, 3, 0, 2, 1).reshape(P, K, UN - UA)
        a = np.concatenate([first, second], axis=2).reshape(P, K * UN)
    elif tail in ("Ds", "dt_projs_bias"):
        a = a.reshape(K, DI).T
    elif tail == "pf_b2":
        a = a.reshape(K)
    else:
        a = a.reshape(-1, 1)
    return np.ascontiguousarray(a)


def kernel(**inputs):
    import concourse.bacc as bacc
    from concourse.bass_utils import run_bass_kernel_spmd

    nc = bacc.Bacc("TRN2", target_bir_lowering=False, num_devices=1)
    arrays, t_in = {}, {}
    for name, a in {**{n: laid_out(n, v) for n, v in inputs.items()}, **constants()}.items():
        arrays["in_" + name] = a
        t_in[name] = nc.dram_tensor("in_" + name, a.shape, mybir.dt.from_np(a.dtype), kind="ExternalInput").ap()
    B = arrays["in_x"].shape[0]
    out = nc.dram_tensor("out_x", [B, DM, L], F32, kind="ExternalOutput").ap()
    build(nc, B, LAYERS, t_in, out)
    r = run_bass_kernel_spmd(nc, [arrays], core_ids=[0])
    return np.ascontiguousarray(r.results[0]["out_x"].transpose(0, 2, 1)).reshape(B, HH, WW, DM)
```

```python
from contextlib import ExitStack

import numpy as np

import concourse.bass as bass
from concourse import mybir

ALU = mybir.AluOpType
ACT = mybir.ActivationFunctionType
AX_X = mybir.AxisListType.X
F32 = mybir.dt.float32
F32R = mybir.dt.float32r
U32 = mybir.dt.uint32

P = 128
HH = WW = 64
L = HH * WW
DM = 96
DI = 192
DB = DI - P
K = 4
N = 16
R = 6
XD = R + 2 * N
G8 = P // N
UN = DI // G8
UA = P // G8
CH = 1024
NC = L // CH
SL = 512
NS = L // SL
BLK = L // P
RDA = 4
RH = 8
LEAD = 5
Z_AT = (6, 16)
ACT_STEPS = {6: [("soft", 0, 0)], 8: [("split", 2), ("soft", 0, 1)], 9: [("soft", 0, 2)], 10: [("soft", 0, 3)],
             11: [("soft", 0, 4)], 16: [("soft", 1, 0)], 17: [("soft", 1, 1)], 18: [("soft", 1, 2), ("split", 0)],
             19: [("soft", 1, 3)], 20: [("split", 1)], 21: [("soft", 1, 4)]}
REST_AT, DU_B_AT, OUT_A_AT = (10, 21), 6, 22
POOL_STEPS = {7: [("split", 2)], 10: [("soft", 0, 0)], 12: [("soft", 0, 1)], 14: [("soft", 0, 2)], 15: [("split", 0)],
              18: [("split", 1)], 22: [("soft", 1, 0)], 25: [("soft", 1, 1)]}
CREDIT = 32
PADW = WW + 2

LAYERS = [
    dict(name="L0_conv", xproj="x_proj_w", dtw="dt_projs_w", g="norm_w", b="norm_b", eps=1e-6, dirs=["n", "w", "rn", "rw"]),
    dict(name="L1_conv", xproj="x_proj_weight", dtw="dt_projs_weight", g="ln_g", b="ln_b", eps=1e-5, dirs=["g"] * 4),
    dict(name="L2_conv", xproj="x_proj_weight", dtw="dt_projs_weight", g="ln_gamma", b="ln_beta", eps=1e-5, dirs=["n", "w", "rn", "rw"]),
    dict(name="L3_conv", xproj="x_proj_weight", dtw="dt_projs_weight", g="ln_gamma", b="ln_beta", eps=1e-5, dirs=["n", "rn", "w", "rw"]),
]


def unit_place(t):
    if t < UA:
        return True, t % 4, t // 4
    return False, (t - UA) % 2, (t - UA) // 2


def by_columns(ap):
    return ap.rearrange("p (h w) -> p w h", w=WW)


def span(i, n):
    return slice(i * n, (i + 1) * n) if isinstance(i, int) else bass.ds(i * n, n)


def by_order(spec):
    d = spec["dirs"]
    return list(range(K)) if d[0] == "g" else [d.index(kind) for kind in ("n", "rn", "w", "rw")]


def build(nc, B, layers, t_in, out):
    ctx = ExitStack()
    with ctx:
        def sb(name, shape, dt=F32):
            return ctx.enter_context(nc.sbuf_tensor(name, shape, dt))

        def sem(name):
            return ctx.enter_context(nc.semaphore(name))

        def dram(name, shape):
            return nc.dram_tensor(name, shape, F32, kind="Internal").ap()

        stream = [dram(f"stream{i}", [B, DM, L]) for i in range(len(layers) - 1)]
        xs_d = dram("xs_by_direction", [K, DI, L])
        xd_d = dram("xproj_by_direction", [K, XD, L])
        xr_d = dram("xproj_reversed", [K, XD, L])
        y_d = dram("y_by_direction", [K, DI, L])
        xtok_d = dram("x_tokens", [L, DI])
        ytok_d = [dram(f"y_tokens{k}", [L, DI]) for k in range(K)]

        w_in = sb("w_in", [DM, 2 * DI])
        w_conv = sb("w_conv", [DM, 9 * DI])
        w_xpA = sb("w_xprojA", [P, K * XD])
        w_xpB = sb("w_xprojB", [DB, K * XD])
        w_dt = sb("w_dt", [P, K * DI])
        rank = sb("rank", [P, CH])[:]
        a_neg = sb("a_neg", [P, K * UN])
        y_sum = sb("y_sumA", [P, L])[:], sb("y_sumB", [P, L])[:]
        vecA = sb("channel_vectorsA", [P, 16])
        vecB = sb("channel_vectorsB", [DB, 16])
        V_D, V_DTB, V_CB, V_G, V_B, V_DS = 0, 4, 8, 9, 10, 13
        w_outA = sb("w_outA", [P, DM])
        w_outB = sb("w_outB", [DB, DM])
        ident = sb("identity", [P, P])
        spread_r = sb("spread", [P, 4 * 4 * P], F32R)
        gather8 = sb("gather8", [P, 4 * 32])
        mean192 = sb("mean192", [P, P])
        mean3 = sb("mean3", [DM, DM])
        carry = sb("carry", [P, K * UN])
        gn_s = sb("gn_statistics", [DM, 6 * NS])
        gn_v = sb("gn_values", [DM, 16])
        dir_b = sb("direction_bias", [XD, K])
        order = sb("order", [P, K * BLK], U32)
        w_pos = sb("w_pos", [P, K * BLK])
        pf = sb("pf_weights", [P, 64])

        SHARED = 36 * CH
        with nc.sbuf_tensor("split_parts", [P, 12 * CH], F32R) as parts:
            pass
        arena = sb("arena", [P, SHARED])
        at = [0]

        def place(n, start=None):
            if start is not None:
                at[0] = start
            a = arena[:, at[0]:at[0] + n]
            at[0] += n
            return a

        hi, lo = {}, {}
        for i, tile in enumerate(("dtA", "duA", "mixB")):
            hi[tile] = [parts[:, (6 * par + 2 * i) * CH:(6 * par + 2 * i + 1) * CH] for par in range(2)]
            lo[tile] = [parts[:, (6 * par + 2 * i + 1) * CH:(6 * par + 2 * i + 2) * CH] for par in range(2)]
        decay = [place(CH, 12 * CH)] + [place(CH) for _ in range(RDA - 1)]
        state = [place(CH) for _ in range(RH)]
        xs_one = place(CH), place(CH)
        bt, ct = [place(CH)], [place(CH)]
        rz, az = zip(*[(place(CH), place(CH)) for _ in range(2)])
        bt.append(place(CH))
        ct.append(place(CH))
        wz, lz = place(CH), place(CH)
        assert at[0] == SHARED
        xs_two = y_sum[0][:, 0:CH], y_sum[1][:, 0:CH]
        yoA, yoB = y_sum[0][:, CH:2 * CH], y_sum[1][:, CH:2 * CH]
        xcA, xcB = place(L, 0), place(L)
        wA, wB = place(L), place(L)
        xdt = [place(L), place(L)]
        x_in = place(L)
        xn = place(PADW * PADW)
        xn_img = xn[0:DM, :].rearrange("p (h w) -> p h w", w=PADW)
        xdr = [place(L, 6 * L), place(L)]
        tok_x = place(BLK * DI, 2 * L)
        tok_g = [place(BLK * DI, 0)]
        permA, permB = zip(*[(place(L), place(L)) for _ in range(2)])
        xdt_tab = [place(L), place(L)]
        tok_g.append(place(BLK * DI))
        x_all = place(L, 7 * L)
        xg = place(L, 0)
        gates = place(L), place(L)
        sq = [place(2 * SL, 3 * L), place(2 * SL)]
        rs = [place(SL) for _ in range(3)]
        xout = [place(SL) for _ in range(2)]
        yin = [(place(L, 0), place(L)), (place(L), place(L))]
        tok_o = [place(BLK * DI), place(BLK * DI)]
        ytok = [place(BLK * DI, 0)] + [place(BLK * DI) for _ in range(K - 1)]
        gates_tab = place(L, 0), place(L)
        xg_tab = place(L)
        spread = place(4 * 4 * P, 0)
        cw_rows = place(9 * DI, 2048)
        coords = place(K * L, 4096)
        hid = [place(SL), place(SL)]
        logit = [place(4 * P) for _ in range(3)]
        red = [place(P) for _ in range(3)]

        ps = ctx.enter_context(nc.psum_tensor("banks", [P, 8, 512], F32))

        def bank(i, rows=P, cols=512, row0=0):
            return ps[row0:row0 + rows, i, 0:cols]

        ps_dt = ps[:, 0:2, :].rearrange("p a b -> p (a b)")
        ps_du = [ps[:, 2 + 2 * i:4 + 2 * i, :].rearrange("p a b -> p (a b)") for i in range(2)]
        ps_y = ps[:, 6:8, :].rearrange("p a b -> p (a b)")

        class Count:

            def __init__(self, c, m, k):
                self.c, self.m, self.k = (c, m, k) if not isinstance(c, int) else (None, 0, c * m + k)

            def __add__(self, n):
                return Count(self.c, self.m, self.k + n) if self.c is not None else Count(0, 0, self.k + n)

            def __sub__(self, n):
                return self + -n

            def __mul__(self, n):
                return Count(self.c, self.m * n, self.k * n) if self.c is not None else Count(0, 0, self.k * n)

        class Signal:

            def __init__(self, name, per, credit=CREDIT):
                self.h, self.per, self.credit = sem(name), per, credit

            def at(self, gb, n):
                b, g0 = gb
                n = n if isinstance(n, Count) else Count(0, 0, n)
                v = g0 * self.per + n.k + self.credit
                assert v >= 0
                if n.c is not None:
                    v = n.c * n.m + v
                return b * self.per + v

        CHK = K * NC
        CONV_ENDS = [4 * (i // 3) + (1, 2, 4)[i % 3] for i in range(3 * NS // 2)]
        const_in = sem("const_in")
        const_ok = sem("const_ok")
        wts_in = sem("wts_in")
        wts_ok = sem("wts_ok")
        init_dve = sem("init_dve")
        setup_dve = sem("setup_dve")
        setup_exp = sem("setup_exp")
        setup_pe = sem("setup_pe")
        setup_act = sem("setup_act")
        step_done = {e: sem(f"step_done_{n}") for e, n in ((nc.vector, "dve"), (nc.tensor, "pe"), (nc.gpsimd, "pool"), (nc.sync, "sp"))}
        x_ld = Signal("x_loaded", 16, 0)
        xz = Signal("xn_zeroed", 1)
        gn_dve = Signal("gn_dve", 13)
        gn_pe = Signal("gn_grouped", 2)
        gn_act = Signal("gn_act", 2)
        cv_pe = Signal("conv_summed", 3 * NS // 2)
        cv_act = Signal("conv_active", 2 * NS)
        pm_dve = Signal("orderA", K)
        pm_act = Signal("orderB", K)
        xp_pe = Signal("xproj_summed", K * NS)
        xp_dve = Signal("xproj_copied", K * NS)
        pre_st = [Signal(f"pre_stored{i}", 64, 0) for i in range(2)]
        xr_st = Signal("reversed_stored", 4 * 16, 0)
        tab_st = [Signal(f"gathered_stored{i}", 2 * 48, 0) for i in range(2)]
        ys0 = Signal("y_begun", 2)
        ld_all = [Signal(f"chunk_loaded{i}", CHK // 2 * 64, 0) for i in range(2)]
        ld_mix = [Signal(f"chunk_loaded_mixed{i}", CHK // 2 * (2 + 2 * K) * 16, 0) for i in range(2)]
        ld_r = Signal("rank_loaded", CHK * 16, 0)
        dt_f = Signal("dt_spread", CHK * UN)
        du_f = Signal("du_spread", CHK * UN)
        ex = Signal("decay_ready", CHK * UN)
        dbu = Signal("dbu_ready", CHK * UN)
        sc = Signal("scanned", CHK * UN)
        ca = Signal("carry_kept", CHK * UN)
        pr = Signal("times_c", CHK * UN)
        yq = Signal("y_summed", CHK * 6)
        ev = Signal("y_out", CHK * 2)
        stA = Signal("yA_stored", CHK * 16)
        stB = Signal("yB_stored", CHK * 16)
        z_pe = Signal("z_ready", CHK * 2)
        z_act = Signal("z_taken", CHK * 2)
        sp_a = Signal("softplus_abs", CHK * 2)
        sp_e = Signal("softplus_exp", CHK * 2)
        sp_w = Signal("softplus_one_plus", CHK * 2)
        sp_l = Signal("softplus_log", CHK * 2)
        sp_r = Signal("softplus_rest", CHK * 2)
        sp_s = Signal("softplus_partial", CHK * 2)
        dt_ok = Signal("dt_ready", CHK * 2)
        du_ok = Signal("du_ready", CHK * 2)
        hi_ok = Signal("hi_ready", CHK * 3)
        lo_ok = Signal("lo_ready", CHK * 3)
        cz = Signal("carry_zeroed", 1)
        x_again = Signal("x_loaded_again", 16, 0)
        xg_ok = Signal("x_normed_again", 1)
        zz_pe = Signal("gate_summed", 3 * NS // 2)
        zz_act = Signal("gate_ready", 2 * NS)
        mu_pe = Signal("mean_ready", NS)
        yc = Signal("y_centred", NS)
        sq_act = Signal("squares_ready", NS)
        va_pe = Signal("variance_ready", NS)
        ln_act = Signal("log_variance", NS)
        rs_act = Signal("rstd_ready", NS)
        yn = Signal("y_normed", NS)
        af = Signal("y_affine", NS)
        gt = Signal("y_gated", NS)
        op_pe = Signal("out_projected", NS)
        xo = Signal("x_out", NS)
        xo_st = [Signal(f"x_stored{i}", NS // 2 * 16) for i in range(2)]
        tk_pe = Signal("tokens_turned", BLK // 2)
        tk_cp = Signal("tokens_copied", BLK // 2)
        tk_st = Signal("tokens_stored", 4 * 16, 0)
        tg = [Signal(f"tokens_gathered{i}", K // 2 * BLK * 16, 0) for i in range(2)]
        pm_cpA = Signal("gatheredA_copied", K * NS)
        pm_cpB = Signal("gatheredB_copied", K * NS)
        ga_pe = Signal("gatheredA_turned", K * NS)
        gb_pe = Signal("gatheredB_turned", K * NS)
        yt_ld = [Signal(f"scan_y_loaded{i}", 2 * 32, 0) for i in range(2)]
        yt_pe = Signal("y_tokens_turned", K * BLK // 2)
        yt_act = Signal("y_tokens_weighted", K * BLK // 2)
        ys_st = [Signal(f"y_tokens_stored{k}", BLK * 16, 0) for k in range(K)]
        yr_ld = Signal("y_tokens_loaded", K * 16, 0)
        yr_ad = Signal("y_tokens_added", 3)
        yb_pe = Signal("y_turned_back", 2 * NS)
        yb_cp = Signal("y_back", 2 * NS)

        block = ctx.enter_context(nc.Block())
        is_tab = [s["dirs"][0] == "g" for s in layers]
        mixed = [s["name"] == "L2_conv" for s in layers]
        counts = [sum(30 if q else 24 for q in is_tab[:i + 1]) for i in range(len(layers))]
        ready = [sum(2 + K if q else 4 for q in is_tab[:i + 1]) for i in range(len(layers))]

        def reverse(kind):
            return "r" in kind

        def stored(kind):
            return int("w" in kind)

        def place_of(c, kind):
            return c * -1 + (NC - 1) if reverse(kind) else c

        def x_tiles(tab, k):
            return (xs_one, xs_two)[k % 2 if tab else 0]

        def ln_eps(li, rows=P):
            return vecA[0:rows, 11:12] if layers[li]["eps"] == 1e-6 else vecA[0:rows, 12:13]

        def per_layer():
            for i, spec in enumerate(layers):
                yield i, spec, i * B, spec["dirs"][0] == "g"

        def loaded(eng, li, b, c, k):
            s, one = (ld_mix, (2 + 2 * K) * 16) if mixed[li] else (ld_all, 64)
            alike = sum(q == mixed[li] for q in mixed[:li])
            eng.wait_ge(s[k % 2].h, s[k % 2].at((b, alike * B), Count(c, 2 * one, (k // 2 + 1) * one)))

        def nxt(c, k):
            return (c, k + 1) if k < K - 1 else (c + 1, 0)

        def chunks(eng, body):
            with eng.Fori(0, NC - 1) as c:
                for k in range(K):
                    body(c, k, False)
            for k in range(K):
                body(NC - 1, k, k == K - 1)

        def uno(c, k, t):
            return Count(c, K * UN, k * UN + t)

        def cno(c, k):
            return Count(c, K, k)

        def passed(eng):
            eng.sem_inc(step_done[eng], 1)

        def credit(eng, *signals):
            for s in signals:
                eng.sem_inc(s.h, CREDIT)

        @block.sync
        def _(sp):
            credit(sp, *xo_st, stA, stB)
            sp.wait_ge(init_dve, 1)
            for dst, src in ((ident[:], t_in["c_ident"]), (spread, t_in["c_spread"]), (gather8[:], t_in["c_gather8"]),
                             (mean192[:], t_in["c_mean192"]), (mean3[:], t_in["c_mean3"]), (order[:], t_in["c_order"])):
                sp.dma_start(dst, src).then_inc(const_in, 16)

            for li, spec, g0, tab in per_layer():
                src_x = t_in["x"] if li == 0 else stream[li - 1]
                dst_x = out if li == len(layers) - 1 else stream[li]
                nm = spec["name"] + "_"
                if li:
                    for i in range(2):
                        sp.wait_ge(xo_st[i].h, xo_st[i].at((0, g0), 0))
                loads = [(w_in[:], t_in[nm + "in_proj_w"]),
                         (cw_rows[0:DM, :], t_in[nm + "conv_w"].unsqueeze(0).broadcast_to([DM, 9 * DI])),
                         (w_dt[0:R, :], t_in[nm + spec["dtw"]]), (a_neg[:], t_in[nm + "A_logs"]),
                         (w_outA[:], t_in[nm + "out_proj_w"][0:P, :]), (w_outB[:], t_in[nm + "out_proj_w"][P:DI, :])]
                for col, name, m in ((V_D, "Ds", K), (V_DTB, "dt_projs_bias", K), (V_CB, "conv_b", 1),
                                     (V_G, spec["g"], 1), (V_B, spec["b"], 1)):
                    loads.append((vecA[:, col:col + m], t_in[nm + name][0:P, :]))
                    loads.append((vecB[:, col:col + m], t_in[nm + name][P:DI, :]))
                for j, k in enumerate(by_order(spec)):
                    for dst, rows in ((w_xpA, slice(0, P)), (w_xpB, slice(P, DI))):
                        loads.append((dst[:, j * XD:(j + 1) * XD], t_in[nm + spec["xproj"]][rows, k * XD:(k + 1) * XD]))
                if tab:
                    loads += [(dir_b[R:R + N, :], t_in[nm + "direction_Bs"]),
                              (coords[0:2, :], t_in["c_coords"]),
                              (pf[0:2, 0:32], t_in[nm + "pf_w1"]), (pf[0:32, 32:33], t_in[nm + "pf_b1"]),
                              (pf[0:32, 36:40], t_in[nm + "pf_w2"]),
                              (pf[:, 40:44], t_in[nm + "pf_b2"].unsqueeze(0).broadcast_to([P, K]))]
                for dst, src in loads:
                    sp.dma_start(dst, src).then_inc(wts_in, 16)
                sp.wait_ge(wts_ok, ready[li])

                def x_of(b):
                    sp.dma_start(x_in[0:DM, :], src_x[b]).then_inc(x_ld.h, 16)

                def element(b, last_one):
                    gb, tb, nb = (b, g0), (b, 0), (b, g0 - B * sum(is_tab[:li]))
                    ld = ld_mix if mixed[li] else ld_all

                    def load(c, k):
                        par = k % 2
                        sp.wait_ge(z_pe.h, z_pe.at(gb, cno(c, k) * 2))
                        passed(sp)
                        kind = spec["dirs"][k]
                        cols = span(place_of(c, kind), CH)
                        sp.dma_start(rank[0:R, :], xd_d[k, 0:R, cols]).then_inc(ld_r.h, 16)
                        sp.wait_ge(ev.h, ev.at(gb, (cno(c, k) - 1) * 2))
                        passed(sp)
                        sp.wait_ge(pr.h, pr.at(gb, (cno(c, k) - 1) * UN))
                        passed(sp)
                        sp.wait_ge(du_ok.h, du_ok.at(gb, cno(c, k) * 2))
                        passed(sp)
                        src, (xA, xB) = k if tab else stored(kind), x_tiles(tab, k)
                        sp.dma_start(xA, xs_d[src, 0:P, cols]).then_inc(ld[par].h, 16)
                        sp.dma_start(xB[0:DB, :], xs_d[src, P:DI, cols]).then_inc(ld[par].h, 16)
                        for dst, row in ((bt[par], R), (ct[par], R + N)):
                            if mixed[li]:
                                for m in range(K):
                                    alike = reverse(spec["dirs"][m]) == reverse(kind)
                                    src = (xd_d if alike else xr_d)[m, row:row + N, cols].unsqueeze(1).broadcast_to([N, G8 // K, CH])
                                    sp.dma_start(dst[m:P:K, :], src).then_inc(ld[par].h, 16)
                            else:
                                src = xd_d[k, row:row + N, cols].unsqueeze(1).broadcast_to([N, G8, CH])
                                sp.dma_start(dst, src).then_inc(ld[par].h, 16)

                    if tab:
                        for q in range(4):
                            blocks = slice(q * BLK // 4, (q + 1) * BLK // 4)
                            sp.wait_ge(tk_cp.h, tk_cp.at(tb, (q + 1) * BLK // 8))
                            sp.dma_start(xtok_d.rearrange("(n p) d -> p n d", p=P)[:, blocks, :],
                                         tok_x.rearrange("p (n d) -> p n d", d=DI)[:, blocks, :]).then_inc(tk_st.h, 16)
                        for k in range(K):
                            sp.wait_ge(pm_dve.h, pm_dve.at(gb, k + 1))
                            sp.wait_ge(pm_act.h, pm_act.at(gb, k + 1))
                            sp.dma_start(xs_d[k, 0:P, :], permA[k % 2]).then_inc(tab_st[k % 2].h, 16)
                            sp.dma_start(xs_d[k, P:DI, :], permB[k % 2][0:DB, :]).then_inc(tab_st[k % 2].h, 16)
                            sp.wait_ge(xp_dve.h, xp_dve.at(gb, (k + 1) * NS))
                            sp.dma_start(xd_d[k], xdt_tab[k % 2][0:XD, :]).then_inc(tab_st[k % 2].h, 16)
                        stores = [(q, tb, 96) for q in tab_st]
                    else:
                        sp.wait_ge(cv_act.h, cv_act.at(gb, 2 * NS))
                        sp.dma_start(xs_d[0, 0:P, :], xcA).then_inc(pre_st[0].h, 16)
                        sp.dma_start(xs_d[0, P:DI, :], xcB[0:DB, :]).then_inc(pre_st[0].h, 16)
                        for o in range(2):
                            if o == 1:
                                if not mixed[li]:
                                    sp.wait_ge(pre_st[0].h, pre_st[0].at(nb, 64))
                                    passed(sp)
                                    load(0, 0)
                                sp.wait_ge(pm_dve.h, pm_dve.at(gb, K))
                                sp.dma_start(xs_d[1, 0:P, :], wA).then_inc(pre_st[1].h, 16)
                                sp.wait_ge(pm_act.h, pm_act.at(gb, K))
                                sp.dma_start(xs_d[1, P:DI, :], wB[0:DB, :]).then_inc(pre_st[1].h, 16)
                            sp.wait_ge(xp_dve.h, xp_dve.at(gb, 2 * (o + 1) * NS))
                            for j, k in enumerate(by_order(spec)[2 * o:2 * o + 2]):
                                sp.dma_start(xd_d[k], xdt[o][j * XD:(j + 1) * XD, :]).then_inc(pre_st[o].h, 16)
                                if mixed[li]:
                                    sp.dma_start(xr_d[k], xdr[o][j * XD:(j + 1) * XD, :]).then_inc(xr_st.h, 16)
                        stores = [(q, nb, 64) for q in pre_st] + ([(xr_st, tb, 64)] if mixed[li] else [])
                    for q, base, n in stores:
                        sp.wait_ge(q.h, q.at(base, n))
                        passed(sp)

                    def body(c, k, last):
                        if not last:
                            load(*nxt(c, k))
                        if last:
                            sp.wait_ge(lo_ok.h, lo_ok.at(gb, CHK * 3))
                            passed(sp)
                            sp.dma_start(x_all[0:DM, :], src_x[b]).then_inc(x_again.h, 16)
                        if not tab:
                            return
                        cols = span(c, CH)
                        sp.wait_ge(ev.h, ev.at(gb, cno(c, k) * 2 + 1))
                        passed(sp)
                        sp.dma_start(y_d[k, 0:P, cols], yoA).then_inc(stA.h, 16)
                        sp.wait_ge(ev.h, ev.at(gb, cno(c, k) * 2 + 2))
                        passed(sp)
                        sp.dma_start(y_d[k, P:DI, cols], yoB[0:DB, :]).then_inc(stB.h, 16)

                    if tab or mixed[li]:
                        load(0, 0)
                    chunks(sp, body)

                    sp.wait_ge(ca.h, ca.at(gb, CHK * UN))
                    passed(sp)
                    if tab:
                        sp.wait_ge(stA.h, stA.at(tb, CHK * 16))
                        passed(sp)
                        sp.wait_ge(stB.h, stB.at(tb, CHK * 16))
                        passed(sp)
                        for k in range(K):
                            if k >= 2:
                                sp.wait_ge(yt_pe.h, yt_pe.at(tb, (k - 1) * BLK // 2))
                            sp.dma_start(yin[k % 2][0], y_d[k, 0:P, :]).then_inc(yt_ld[k % 2].h, 16)
                            sp.dma_start(yin[k % 2][1][0:DB, :], y_d[k, P:DI, :]).then_inc(yt_ld[k % 2].h, 16)
                        sp.wait_ge(yt_pe.h, yt_pe.at(tb, K * BLK // 2))
                        for k in range(K):
                            if k == 2:
                                for i in range(2, K):
                                    sp.wait_ge(ys_st[i].h, ys_st[i].at(tb, BLK * 16))
                            sp.wait_ge(ys_st[k].h, ys_st[k].at(tb, BLK * 16))
                            sp.dma_start(ytok[k].rearrange("p (n d) -> p n d", d=DI),
                                         ytok_d[k].rearrange("(n p) d -> p n d", p=P)).then_inc(yr_ld.h, 16)
                    if not last_one:
                        sp.wait_ge(pr.h, pr.at(gb, CHK * UN))
                        passed(sp)
                        x_of(b + 1)
                    for s in range(NS):
                        sp.wait_ge(xo.h, xo.at(gb, s + 1))
                        passed(sp)
                        sp.dma_start(dst_x[b][:, s * SL:(s + 1) * SL], xout[s % 2][0:DM, :]).then_inc(xo_st[s % 2].h, 16)
                x_of(0)
                if B > 1:
                    with sp.Fori(0, B - 1) as b:
                        element(b, False)
                element(B - 1, True)
            for i in range(2):
                sp.wait_ge(xo_st[i].h, xo_st[i].at((0, len(layers) * B), 0))

        @block.tensor
        def _(pe):
            credit(pe, gn_pe, cv_pe, xp_pe, dt_f, du_f, yq, z_pe, zz_pe, mu_pe, va_pe, op_pe,
                   tk_pe, ga_pe, gb_pe, yt_pe, yb_pe)
            pe.wait_ge(const_ok, 1)
            for li, spec, g0, tab in per_layer():
                if tab:
                    pe.wait_ge(wts_in, 16 * counts[li])
                    for i in range(K * NS):
                        if i >= 2:
                            pe.wait_ge(setup_act, i - 1)
                        pe.matmul(bank(i % 2, 32), pf[0:2, 0:32], coords[0:2, i * SL:(i + 1) * SL],
                                  start=True, stop=True).then_inc(setup_pe, 1)
                        pe.wait_ge(setup_act, i + 1)
                        for q in range(4):
                            blk = 4 * i + q
                            mm = pe.matmul(ps[:, 2, 4 * blk:4 * blk + 4], hid[i % 2][0:32, q * P:(q + 1) * P],
                                           pf[0:32, 36:40], start=True, stop=True)
                        mm.then_inc(setup_pe, 1)
                pe.wait_ge(wts_ok, ready[li])
                with pe.Fori(0, B) as b:
                    gb, tb, nb = (b, g0), (b, 0), (b, g0 - B * sum(is_tab[:li]))
                    for i in range(2):
                        pe.wait_ge(gn_dve.h, gn_dve.at(gb, (9, 12)[i]))
                        pe.matmul(ps[0:DM, i, 0:1], mean3[:], gn_v[:, 3 * i:3 * i + 1], start=True, stop=True).then_inc(gn_pe.h, 1)
                    pe.wait_ge(gn_dve.h, gn_dve.at(gb, 13))
                    rows = SL // WW

                    def conv(i, outs):
                        if i >= 4:
                            pe.wait_ge(cv_act.h, cv_act.at(gb, CONV_ENDS[i - 4]))
                        for tap in range(9):
                            dy, dx = divmod(tap, 3)
                            for p0, m, d0, s in outs:
                                mm = pe.matmul(bank(i % 4, m, SL, p0), w_conv[:, tap * DI + d0:tap * DI + d0 + m],
                                               xn_img[:, s * rows + dy:s * rows + dy + rows, dx:dx + WW],
                                               start=tap == 0, stop=tap == 8)
                        mm.then_inc(cv_pe.h, 1)

                    def xproj(o, s, A, B):
                        i = o * NS + s
                        if i >= 4:
                            pe.wait_ge(xp_dve.h, xp_dve.at(gb, 2 * (i - 3)))
                        out_rows, w = bank(4 + i % 4, 2 * XD), slice(2 * o * XD, 2 * (o + 1) * XD)
                        pe.matmul(out_rows, w_xpA[:, w], A, start=True, stop=False)
                        pe.matmul(out_rows, w_xpB[:, w], B, start=False, stop=True).then_inc(xp_pe.h, 2)

                    def xproj_rows(pair):
                        pe.wait_ge(cv_act.h, cv_act.at(gb, CONV_ENDS[3 * pair + 2]))
                        for s in (2 * pair, 2 * pair + 1):
                            cols = slice(s * SL, (s + 1) * SL)
                            xproj(0, s, xcA[:, cols], xcB[0:DB, cols])

                    def to_tokens(pair):
                        pe.wait_ge(cv_act.h, cv_act.at(gb, CONV_ENDS[3 * pair + 2]))
                        per = BLK // NS
                        for i in range(pair * per, (pair + 1) * per):
                            if i >= 4:
                                pe.wait_ge(tk_cp.h, tk_cp.at(tb, i - 3))
                            for q in range(2):
                                blk = 2 * i + q
                                pe.transpose(ps[:, 4 + i % 4, q * DI:q * DI + P], xcA[:, blk * P:(blk + 1) * P], ident[:])
                                mm = pe.transpose(ps[:, 4 + i % 4, q * DI + P:(q + 1) * DI], xcB[0:DB, blk * P:(blk + 1) * P],
                                                  ident[0:DB, 0:DB])
                            mm.then_inc(tk_pe.h, 1)

                    for pair in range(NS // 2):
                        s = 2 * pair
                        conv(3 * pair, [(0, P, 0, s)])
                        conv(3 * pair + 1, [(0, P, 0, s + 1)])
                        conv(3 * pair + 2, [(0, DB, P, s), (DB, DB, P, s + 1)])
                        if pair:
                            (to_tokens if tab else xproj_rows)(pair - 1)
                    pe.wait_ge(cv_act.h, cv_act.at(gb, 2 * NS))
                    if tab:
                        to_tokens(NS // 2 - 1)
                    else:
                        xproj_rows(NS // 2 - 1)
                        for s in range(NS):
                            cs = slice(s * rows, (s + 1) * rows)
                            xproj(1, s, by_columns(xcA)[:, cs, :], by_columns(xcB[0:DB, :])[:, cs, :])
                    for k in range(K if tab else 0):
                        pe.wait_ge(tg[k % 2].h, tg[k % 2].at(tb, (k // 2 + 1) * BLK * 16))
                        if k == 0:
                            pe.wait_ge(tk_cp.h, tk_cp.at(tb, BLK // 2))
                        for m in range(NS):
                            i = k * NS + m
                            if m >= 2:
                                pe.wait_ge(pm_cpA.h, pm_cpA.at(tb, i - 1))
                                pe.wait_ge(pm_cpB.h, pm_cpB.at(tb, i - 1))
                            elif k:
                                pe.wait_ge(pm_dve.h, pm_dve.at(gb, k))
                                pe.wait_ge(pm_act.h, pm_act.at(gb, k))
                            for q in range(4):
                                blk = 4 * m + q
                                mm = pe.transpose(ps[:, m % 2, q * P:(q + 1) * P], tok_g[k % 2][:, blk * DI:blk * DI + P], ident[:])
                            mm.then_inc(ga_pe.h, 1)
                            passed(pe)
                            for q in range(4):
                                blk = 4 * m + q
                                mm = pe.transpose(ps[0:DB, 2 + m % 2, q * P:(q + 1) * P],
                                                  tok_g[k % 2][:, blk * DI + P:(blk + 1) * DI], ident[:])
                            mm.then_inc(gb_pe.h, 1)
                        a, bb = permA[k % 2], permB[k % 2]
                        pe.wait_ge(pm_dve.h, pm_dve.at(gb, k + 1))
                        pe.wait_ge(pm_act.h, pm_act.at(gb, k + 1))
                        for s in range(NS):
                            i = k * NS + s
                            if i >= 4:
                                pe.wait_ge(xp_dve.h, xp_dve.at(gb, i - 3))
                            o = bank(4 + i % 4, XD)
                            pe.matmul(o, w_xpA[:, k * XD:(k + 1) * XD], a[:, s * SL:(s + 1) * SL], start=True, stop=False)
                            pe.matmul(o, w_xpB[:, k * XD:(k + 1) * XD], bb[0:DB, s * SL:(s + 1) * SL],
                                      start=False, stop=True).then_inc(xp_pe.h, 1)
                    pe.wait_ge(xp_dve.h, xp_dve.at(gb, K * NS))

                    def z(c, k, half, spread_so_far):
                        if half == 0:
                            pe.wait_ge(ld_r.h, ld_r.at(gb, (cno(c, k) + 1) * 16))
                        d0, m = (0, P) if half == 0 else (P, DB)
                        pe.wait_ge(ex.h, ex.at(gb, spread_so_far))
                        for h in range(2):
                            mm = pe.matmul(ps_dt[0:m, h * SL:(h + 1) * SL], w_dt[:, k * DI + d0:k * DI + d0 + m],
                                           rank[:, h * SL:(h + 1) * SL], start=True, stop=True)
                        mm.then_inc(z_pe.h, 1)


                    def spread_rows(dst, tile, par, group, part):
                        for h in range(2):
                            for j, src in enumerate((hi[tile][par], lo[tile][par])):
                                v = (group * 4 + part) * P
                                mm = pe.matmul(dst[:, h * SL:(h + 1) * SL], spread_r[:, v:v + P],
                                               src[:, h * SL:(h + 1) * SL], start=j == 0, stop=j == 1)
                        return mm

                    def unit(c, k, t, z_before=None):
                        first, rg, part = unit_place(t)
                        u = uno(c, k, t)
                        if t == 0:
                            pe.wait_ge(lo_ok.h, lo_ok.at(gb, cno(c, k) * 3 + 2))
                        if t == UA:
                            pe.wait_ge(lo_ok.h, lo_ok.at(gb, cno(c, k) * 3 + 3))
                        for what in ("dt", "du") if z_before is None else ("du", "dt"):
                            if what == "dt":
                                pe.wait_ge(ex.h, ex.at(gb, u))
                                if z_before is not None:
                                    pe.wait_ge(z_act.h, z_act.at(gb, z_before))
                                spread_rows(ps_dt, "dtA" if first else "mixB", k % 2, rg, part).then_inc(dt_f.h, 1)
                            else:
                                pe.wait_ge(sc.h, sc.at(gb, u - 1))
                                spread_rows(ps_du[t % 2], "duA" if first else "mixB", k % 2,
                                            rg if first else 2 + rg, part).then_inc(du_f.h, 1)

                    def quad(c, k, m):
                        pe.wait_ge(pr.h, pr.at(gb, uno(c, k, 4 * m + 4)))
                        if m == 0:
                            pe.wait_ge(ev.h, ev.at(gb, cno(c, k) * 2))
                        if m == 4:
                            pe.wait_ge(ev.h, ev.at(gb, cno(c, k) * 2 + 1))
                        for h in range(2):
                            for t in range(4 * m, 4 * m + 4):
                                _, rg, part = unit_place(t)
                                mm = pe.matmul(ps_y[32 * rg:32 * rg + 32, h * SL:(h + 1) * SL],
                                               gather8[:, part * 32:(part + 1) * 32],
                                               state[t % RH][:, h * SL:(h + 1) * SL], start=part == 0, stop=part == 3)
                        mm.then_inc(yq.h, 1)

                    def body(c, k, last):
                        for t in range(LEAD, UN if last else UN + LEAD):
                            if t < UN:
                                z_before = None
                                if not last and t - 1 in Z_AT:
                                    z_before = cno(*nxt(c, k)) * 2 + Z_AT.index(t - 1) + 1
                                unit(c, k, t, z_before)
                            else:
                                unit(*nxt(c, k), t - UN)
                            if not last and t in Z_AT:
                                z(*nxt(c, k), Z_AT.index(t), uno(c, k, t + 1))
                            if t >= 8 and t % 4 == 0:
                                quad(c, k, t // 4 - 2)
                        if last:
                            quad(c, k, 4)
                            quad(c, k, 5)

                    for half in range(2):
                        z(0, 0, half, 0)
                        pe.wait_ge(z_act.h, z_act.at(gb, half + 1))
                    for t in range(LEAD):
                        unit(0, 0, t)
                    chunks(pe, body)

                    if tab:
                        for i in range(K * BLK // 2):
                            k, m = divmod(i, BLK // 2)
                            if i == 0:
                                pe.wait_ge(ev.h, ev.at(gb, CHK * 2))
                            if m == 0:
                                pe.wait_ge(yt_ld[k % 2].h, yt_ld[k % 2].at(tb, (k // 2 + 1) * 32))
                            if i >= 4:
                                pe.wait_ge(yt_act.h, yt_act.at(tb, i - 3))
                            for q in range(2):
                                blk = 2 * m + q
                                pe.transpose(ps[:, i % 4, q * DI:q * DI + P], yin[k % 2][0][:, blk * P:(blk + 1) * P], ident[:])
                                mm = pe.transpose(ps[:, i % 4, q * DI + P:(q + 1) * DI],
                                                  yin[k % 2][1][0:DB, blk * P:(blk + 1) * P], ident[0:DB, 0:DB])
                            mm.then_inc(yt_pe.h, 1)
                        pe.wait_ge(yt_act.h, yt_act.at(tb, K * BLK // 2))
                        pe.wait_ge(yr_ad.h, yr_ad.at(tb, 3))
                        for i in range(2 * NS):
                            m, half = divmod(i, 2)
                            if i >= 4:
                                pe.wait_ge(yb_cp.h, yb_cp.at(tb, i - 3))
                            passed(pe)
                            for q in range(4):
                                blk = 4 * m + q
                                c0, w = (0, P) if half == 0 else (P, DB)
                                mm = pe.transpose(ps[0:w, i % 4, q * P:(q + 1) * P],
                                                  ytok[0][:, blk * DI + c0:blk * DI + c0 + w], ident[:])
                            mm.then_inc(yb_pe.h, 1)
                        pe.wait_ge(yb_cp.h, yb_cp.at(tb, 2 * NS))
                    pe.wait_ge(xg_ok.h, xg_ok.at(gb, 1))
                    pe.wait_ge(ex.h, ex.at(gb, CHK * UN))
                    xg_now = xg_tab if tab else xg
                    for i in range(3 * NS // 2):
                        pair, j = divmod(i, 3)
                        if i == 2:
                            pe.wait_ge(sc.h, sc.at(gb, CHK * UN - 1))
                        if i >= 4:
                            pe.wait_ge(zz_act.h, zz_act.at(gb, CONV_ENDS[i - 4]))
                        s = 2 * pair + (j == 1)
                        for p0, m, d0, q in ([(0, P, DI, s)] if j < 2 else [(0, DB, DI + P, s), (DB, DB, DI + P, s + 1)]):
                            mm = pe.matmul(bank(i % 4, m, SL, p0), w_in[:, d0:d0 + m], xg_now[0:DM, q * SL:(q + 1) * SL],
                                           start=True, stop=True)
                        mm.then_inc(zz_pe.h, 1)
                    pe.wait_ge(ev.h, ev.at(gb, CHK * 2))
                    pe.wait_ge(sc.h, sc.at(gb, CHK * UN))
                    for s in range(NS + 3):
                        if s < NS:
                            if s >= 2:
                                pe.wait_ge(yc.h, yc.at(gb, s - 1))
                            cols = slice(s * SL, (s + 1) * SL)
                            pe.matmul(bank(6 + s % 2), mean192[:], y_sum[0][:, cols], start=True, stop=False)
                            pe.matmul(bank(6 + s % 2), mean192[0:DB, :], y_sum[1][0:DB, cols],
                                      start=False, stop=True).then_inc(mu_pe.h, 1)
                        v = s - 1
                        if 0 <= v < NS:
                            if v == 0:
                                pe.wait_ge(zz_act.h, zz_act.at(gb, 2 * NS))
                            pe.wait_ge(sq_act.h, sq_act.at(gb, v + 1))
                            if v >= 2:
                                pe.wait_ge(ln_act.h, ln_act.at(gb, v - 1))
                            pe.matmul(bank(2 + v % 2), mean192[:], sq[v % 2][:, 0:SL], start=True, stop=False)
                            pe.matmul(bank(2 + v % 2), mean192[0:DB, :], sq[v % 2][0:DB, SL:2 * SL],
                                      start=False, stop=True).then_inc(va_pe.h, 1)
                        o = s - 3
                        if 0 <= o < NS:
                            pe.wait_ge(gt.h, gt.at(gb, o + 1))
                            if o >= 2:
                                pe.wait_ge(xo.h, xo.at(gb, o - 1))
                            cols = slice(o * SL, (o + 1) * SL)
                            pe.matmul(bank(4 + o % 2, DM), w_outA[:], y_sum[0][:, cols], start=True, stop=False)
                            pe.matmul(bank(4 + o % 2, DM), w_outB[:], y_sum[1][0:DB, cols],
                                      start=False, stop=True).then_inc(op_pe.h, 1)
                    pe.wait_ge(xo.h, xo.at(gb, NS))

        @block.scalar
        def _(act):
            credit(act, gn_act, cv_act, pm_act, pm_cpB, ys0, ex, ca, z_act, sp_a, sp_e, sp_w, sp_l, hi_ok,
                   zz_act, sq_act, ln_act, rs_act, af, yt_act)
            for li, spec, g0, tab in per_layer():
                act.wait_ge(wts_in, 16 * counts[li])
                act.activation(a_neg[:], a_neg[:], ACT.Exp).then_inc(setup_exp, 1)
                if tab:
                    for i in range(K * NS):
                        act.wait_ge(setup_pe, 2 * i + 1)
                        if i >= 2:
                            act.wait_ge(setup_pe, 2 * (i - 1))
                        act.activation(hid[i % 2][0:32, :], bank(i % 2, 32), ACT.Gelu, bias=pf[0:32, 32:33]).then_inc(setup_act, 1)
                    act.wait_ge(setup_dve, 3)
                    act.activation(logit[1], logit[1], ACT.Exp).then_inc(setup_exp, 1)
                act.wait_ge(wts_ok, ready[li])
                with act.Fori(0, B) as b:
                    gb, tb, nb = (b, g0), (b, 0), (b, g0 - B * sum(is_tab[:li]))
                    act.preload_act_table_set("natural_log_exp_and_others")
                    act.wait_ge(gn_pe.h, gn_pe.at(gb, 2))
                    act.activation(gn_v[:, 6:7], ps[0:DM, 1, 0:1], ACT.Ln, bias=gn_v[:, 8:9]).then_inc(gn_act.h, 1)
                    act.wait_ge(gn_act.h, gn_act.at(gb, 1))
                    act.activation(gn_v[:, 7:8], gn_v[:, 6:7], ACT.Exp, scale=-0.5).then_inc(gn_act.h, 1)
                    act.wait_ge(xo.h, xo.at(gb, 0))
                    for i in range(3 * NS // 2):
                        act.wait_ge(cv_pe.h, cv_pe.at(gb, i + 1))
                        pair, j = divmod(i, 3)
                        for p0, m, dst, vec, s in ([(0, P, xcA, vecA, 2 * pair + j)] if j < 2 else
                                                   [(q * DB, DB, xcB, vecB, 2 * pair + q) for q in range(2)]):
                            act.activation(dst[0:m, s * SL:(s + 1) * SL], bank(i % 4, m, SL, p0), ACT.Silu,
                                           bias=vec[0:m, V_CB:V_CB + 1]).then_inc(cv_act.h, 1)
                    act.wait_ge(cv_act.h, cv_act.at(gb, 2 * NS))
                    if tab:
                        for k in range(K):
                            if k >= 2:
                                act.wait_ge(tab_st[k % 2].h, tab_st[k % 2].at(tb, 48 * (k // 2)))
                            if k == 0:
                                act.wait_ge(tk_st.h, tk_st.at(tb, 64))
                            for m in range(NS):
                                act.wait_ge(gb_pe.h, gb_pe.at(tb, k * NS + m + 1))
                                act.activation(permB[k % 2][0:DB, m * SL:(m + 1) * SL], bank(2 + m % 2, DB),
                                               ACT.Copy).then_inc(pm_cpB.h, 1)
                            act.wait_ge(pm_cpB.h, pm_cpB.at(tb, (k + 1) * NS))
                            act.sem_inc(pm_act.h, 1)
                    else:
                        act.activation(wB[0:DB, :].rearrange("p (a b) -> p a b", b=HH), by_columns(xcB[0:DB, :]),
                                       ACT.Copy).then_inc(pm_act.h, K)
                        act.activation(y_sum[0], xcA, ACT.Copy, scale=vecA[:, V_DS:V_DS + 1]).then_inc(ys0.h, 1)
                        act.activation(y_sum[1][0:DB, :], xcB[0:DB, :], ACT.Copy,
                                       scale=vecB[:, V_DS:V_DS + 1]).then_inc(ys0.h, 1)

                    act.preload_act_table_set("natural_log_exp_and_others")

                    def decays(c, k, t):
                        u = uno(c, k, t)
                        act.wait_ge(dt_f.h, dt_f.at(gb, u + 1))
                        act.wait_ge(sc.h, sc.at(gb, u - RDA + 1))
                        act.activation(decay[(t) % RDA], ps_dt, ACT.Exp,
                                       scale=a_neg[:, k * UN + t:k * UN + t + 1]).then_inc(ex.h, 1)

                    def keep(c, k, t):
                        act.wait_ge(sc.h, sc.at(gb, uno(c, k, t) + 1))
                        end = 0 if reverse(spec["dirs"][k]) else CH - 1
                        act.activation(carry[:, k * UN + t:k * UN + t + 1], state[t % RH][:, end:end + 1],
                                       ACT.Copy).then_inc(ca.h, 1)

                    def soft(c, k, half, step):
                        m, vec = (P, vecA) if half == 0 else (DB, vecB)
                        n = cno(c, k) * 2 + half
                        bias = vec[:, V_DTB + k:V_DTB + k + 1]
                        if step == 0:
                            act.wait_ge(z_pe.h, z_pe.at(gb, n + 1))
                            act.wait_ge(sp_r.h, sp_r.at(gb, n))
                            act.wait_ge(sp_l.h, sp_l.at(gb, n))
                            act.activation(wz[0:m, :], ps_dt[0:m, :], ACT.Identity, bias=bias).then_inc(z_act.h, 1)
                        elif step == 1:
                            act.wait_ge(z_act.h, z_act.at(gb, n + 1))
                            act.wait_ge(lo_ok.h, lo_ok.at(gb, cno(c, k) * 3 + half - 1))
                            act.activation(rz[half][0:m, :], wz[0:m, :], ACT.Relu)
                            act.activation(az[half][0:m, :], wz[0:m, :], ACT.Abs).then_inc(sp_a.h, 1)
                        elif step == 2:
                            act.wait_ge(sp_a.h, sp_a.at(gb, n + 1))
                            act.activation(az[half][0:m, :], az[half][0:m, :], ACT.Exp, scale=-1.0).then_inc(sp_e.h, 1)
                        elif step == 3:
                            act.wait_ge(sp_e.h, sp_e.at(gb, n + 1))
                            act.activation(wz[0:m, :], az[half][0:m, :], ACT.Identity, bias=1.0).then_inc(sp_w.h, 1)
                        else:
                            act.wait_ge(sp_w.h, sp_w.at(gb, n + 1))
                            act.wait_ge(dt_ok.h, dt_ok.at(gb, n))
                            act.activation(lz[0:m, :], wz[0:m, :], ACT.Ln).then_inc(sp_l.h, 1)

                    def split(c, k, i):
                        s = (dt_ok, du_ok, du_ok)[i]
                        act.wait_ge(s.h, s.at(gb, cno(c, k) * 2 + (1, 1, 2)[i]))
                        act.activation(hi[("dtA", "duA", "mixB")[i]][k % 2], (rz[0], az[0], rz[1])[i], ACT.Copy).then_inc(hi_ok.h, 1)

                    def body(c, k, last):
                        for t in range(LEAD, UN + (2 if last else LEAD)):
                            if t < UN:
                                decays(c, k, t)
                            elif not last:
                                decays(*nxt(c, k), t - UN)
                            if t - 2 < UN:
                                keep(c, k, t - 2)
                            else:
                                keep(*nxt(c, k), t - 2 - UN)
                            for what, *args in ACT_STEPS.get(t, ()):
                                if args == [2]:
                                    split(c, k, 2)
                                elif not last:
                                    (soft if what == "soft" else split)(*nxt(c, k), *args)

                    if tab:
                        for q in tab_st:
                            act.wait_ge(q.h, q.at(tb, 96))
                    for step in range(5):
                        soft(0, 0, 0, step)
                    act.wait_ge(xp_dve.h, xp_dve.at(gb, K * NS))
                    act.wait_ge(pm_dve.h, pm_dve.at(gb, K))
                    if not tab:
                        act.wait_ge(pre_st[0].h, pre_st[0].at(nb, 64))
                    split(0, 0, 0)
                    split(0, 0, 1)
                    for step in range(5):
                        soft(0, 0, 1, step)
                    if not tab:
                        act.wait_ge(pre_st[1].h, pre_st[1].at(nb, 64))
                    for t in range(LEAD):
                        decays(0, 0, t)
                        if t >= 2:
                            keep(0, 0, t - 2)
                    chunks(act, body)

                    if tab:
                        for i in range(K * BLK // 2):
                            k, m = divmod(i, BLK // 2)
                            if m == 0 and k >= 2:
                                act.wait_ge(ys_st[k % 2].h, ys_st[k - 2].at(tb, BLK * 16))
                            act.wait_ge(yt_pe.h, yt_pe.at(tb, i + 1))
                            for q in range(2):
                                blk = 2 * m + q
                                ins = act.activation(tok_o[k % 2][:, blk * DI:(blk + 1) * DI], ps[:, i % 4, q * DI:(q + 1) * DI],
                                                     ACT.Copy, scale=w_pos[:, k * BLK + blk:k * BLK + blk + 1])
                            ins.then_inc(yt_act.h, 1)
                        act.wait_ge(yb_cp.h, yb_cp.at(tb, 2 * NS))
                    act.wait_ge(pr.h, pr.at(gb, CHK * UN))
                    for i in range(3 * NS // 2):
                        act.wait_ge(zz_pe.h, zz_pe.at(gb, i + 1))
                        pair, j = divmod(i, 3)
                        zA, zB = gates_tab if tab else gates
                        for p0, m, dst, s in ([(0, P, zA, 2 * pair + j)] if j < 2 else
                                              [(q * DB, DB, zB, 2 * pair + q) for q in range(2)]):
                            act.activation(dst[0:m, s * SL:(s + 1) * SL], bank(i % 4, m, SL, p0), ACT.Silu).then_inc(zz_act.h, 1)
                    act.preload_act_table_set("natural_log_exp_and_others")
                    for s in range(NS + 2):
                        if s < NS:
                            act.wait_ge(yc.h, yc.at(gb, s + 1))
                            if s >= 2:
                                act.wait_ge(va_pe.h, va_pe.at(gb, s - 1))
                            cols = slice(s * SL, (s + 1) * SL)
                            act.activation(sq[s % 2][:, 0:SL], y_sum[0][:, cols], ACT.Square)
                            act.activation(sq[s % 2][0:DB, SL:2 * SL], y_sum[1][0:DB, cols], ACT.Square).then_inc(sq_act.h, 1)
                        v = s - 1
                        if 0 <= v < NS:
                            act.wait_ge(va_pe.h, va_pe.at(gb, v + 1))
                            if v >= 3:
                                act.wait_ge(yn.h, yn.at(gb, v - 2))
                            act.activation(rs[v % 3], bank(2 + v % 2), ACT.Ln, bias=ln_eps(li)).then_inc(ln_act.h, 1)
                            act.wait_ge(ln_act.h, ln_act.at(gb, v + 1))
                            act.activation(rs[v % 3], rs[v % 3], ACT.Exp, scale=-0.5).then_inc(rs_act.h, 1)
                        a = s - 2
                        if 0 <= a < NS:
                            act.wait_ge(yn.h, yn.at(gb, a + 1))
                            cols = slice(a * SL, (a + 1) * SL)
                            for m, yy, vec in ((P, y_sum[0], vecA), (DB, y_sum[1], vecB)):
                                ins = act.activation(yy[0:m, cols], yy[0:m, cols], ACT.Identity,
                                                     scale=vec[:, V_G:V_G + 1], bias=vec[:, V_B:V_B + 1])
                            ins.then_inc(af.h, 1)

        @block.vector
        def _(dve):
            credit(dve, gn_dve, pm_dve, pm_cpA, xp_dve, dbu, sc, ev, sp_r, cz, xg_ok, yc, yn, xo, yr_ad, yb_cp, tk_cp)
            dve.memset(vecA[:, 11:12], 1e-6)
            dve.memset(vecA[:, 12:13], 1e-5)
            dve.memset(dir_b[:], 0.0)
            dve.memset(w_dt[:], 0.0)
            dve.memset(rank, 0.0)
            dve.memset(gn_v[:, 8:9], 1e-5).then_inc(init_dve, 1)
            dve.wait_ge(const_in, 96)
            dve.tensor_copy(spread_r[:], spread).then_inc(const_ok, 1)
            dve.wait_ge(init_dve, 1)
            for li, spec, g0, tab in per_layer():
                dve.wait_ge(wts_in, 16 * counts[li])
                dve.tensor_tensor(w_conv[:].rearrange("p (t d) -> p t d", d=DI),
                                  cw_rows[0:DM, :].rearrange("p (t d) -> p t d", d=DI),
                                  w_in[:, 0:DI].unsqueeze(1).broadcast_to([DM, 9, DI]), ALU.mult).then_inc(wts_ok, 1)
                exps = li + 1 + sum(is_tab[:li])
                dve.wait_ge(setup_exp, exps)
                dve.tensor_scalar(a_neg[:], a_neg[:], -1.0, None, ALU.mult).then_inc(wts_ok, 1)
                if not tab:
                    for vec in (vecA, vecB):
                        dve.tensor_reduce(vec[:, V_DS:V_DS + 1], vec[:, V_D:V_D + K], AX_X, ALU.add).then_inc(wts_ok, 1)
                if tab:
                    lg = [v.rearrange("p (t k) -> p t k", k=K) for v in logit]
                    dve.wait_ge(setup_pe, 2 * K * NS)
                    dve.tensor_tensor(lg[0], ps[:, 2, :].rearrange("p (t k) -> p t k", k=K),
                                      pf[:, 40:44].unsqueeze(1).broadcast_to([P, P, K]), ALU.add).then_inc(setup_dve, 1)
                    dve.wait_ge(setup_dve, 1)
                    dve.tensor_reduce(red[0], lg[0], AX_X, ALU.max).then_inc(setup_dve, 1)
                    dve.wait_ge(setup_dve, 2)
                    dve.tensor_tensor(lg[1], lg[0], red[0].unsqueeze(2).broadcast_to([P, P, K]), ALU.subtract).then_inc(setup_dve, 1)
                    dve.wait_ge(setup_exp, exps + 1)
                    dve.tensor_reduce(red[1], lg[1], AX_X, ALU.add).then_inc(setup_dve, 1)
                    dve.wait_ge(setup_dve, 4)
                    dve.reciprocal(red[2], red[1]).then_inc(setup_dve, 1)
                    dve.wait_ge(setup_dve, 5)
                    for k in range(K):
                        dve.tensor_tensor(w_pos[:, k * BLK:(k + 1) * BLK], lg[1][:, k * BLK:(k + 1) * BLK, k],
                                          red[2][:, k * BLK:(k + 1) * BLK], ALU.mult).then_inc(wts_ok, 1)
                with dve.Fori(0, B) as b:
                    gb, tb, nb = (b, g0), (b, 0), (b, g0 - B * sum(is_tab[:li]))
                    for i in range(2):
                        dve.wait_ge(xo_st[i].h, xo_st[i].at(gb, 0))
                    dve.wait_ge(x_ld.h, x_ld.at(gb, 16))
                    for s in range(NS):
                        dve.bn_stats(gn_s[:, 6 * s:6 * s + 6], x_in[0:DM, s * SL:(s + 1) * SL]).then_inc(gn_dve.h, 1)
                    dve.wait_ge(gn_dve.h, gn_dve.at(gb, 8))
                    passed(dve)
                    dve.bn_aggr(gn_v[:, 0:2], gn_s[:]).then_inc(gn_dve.h, 1)
                    dve.wait_ge(gn_dve.h, gn_dve.at(gb, 9))
                    dve.wait_ge(gn_pe.h, gn_pe.at(gb, 1))
                    dve.tensor_tensor(gn_v[:, 2:3], gn_v[:, 0:1], ps[0:DM, 0, 0:1], ALU.subtract).then_inc(gn_dve.h, 1)
                    dve.tensor_copy(gn_v[:, 4:5], ps[0:DM, 0, 0:1]).then_inc(gn_dve.h, 1)
                    dve.wait_ge(gn_dve.h, gn_dve.at(gb, 11))
                    dve.scalar_tensor_tensor(gn_v[:, 3:4], gn_v[:, 2:3], gn_v[:, 2:3], gn_v[:, 1:2], ALU.mult, ALU.add).then_inc(gn_dve.h, 1)
                    dve.wait_ge(gn_act.h, gn_act.at(gb, 2))
                    dve.wait_ge(xz.h, xz.at(gb, 1))
                    dve.tensor_scalar(xn_img[:, 1:1 + HH, 1:1 + WW], x_in[0:DM, :].rearrange("p (h w) -> p h w", w=WW),
                                      gn_v[:, 4:5], gn_v[:, 7:8], ALU.subtract, ALU.mult).then_inc(gn_dve.h, 1)
                    if tab:
                        for i in range(BLK // 2):
                            dve.wait_ge(tk_pe.h, tk_pe.at(tb, i + 1))
                            dve.tensor_copy(tok_x[:, 2 * i * DI:(2 * i + 2) * DI], ps[:, 4 + i % 4, 0:2 * DI]).then_inc(tk_cp.h, 1)

                    if tab:
                        for k in range(K):
                            if k >= 2:
                                dve.wait_ge(tab_st[k % 2].h, tab_st[k % 2].at(tb, 48 * (k // 2)))
                            if k == 0:
                                dve.wait_ge(tk_st.h, tk_st.at(tb, 64))
                            for m in range(NS):
                                dve.wait_ge(ga_pe.h, ga_pe.at(tb, k * NS + m + 1))
                                dve.tensor_copy(permA[k % 2][:, m * SL:(m + 1) * SL], bank(m % 2)).then_inc(pm_cpA.h, 1)
                            dve.wait_ge(pm_cpA.h, pm_cpA.at(tb, (k + 1) * NS))
                            dve.sem_inc(pm_dve.h, 1)
                            for s in range(NS):
                                dve.wait_ge(xp_pe.h, xp_pe.at(gb, k * NS + s + 1))
                                dve.tensor_scalar(xdt_tab[k % 2][0:XD, s * SL:(s + 1) * SL], bank(4 + s % 4, XD),
                                                  dir_b[:, k:k + 1], None, ALU.add).then_inc(xp_dve.h, 1)
                    else:
                        for i in range(2 * NS):
                            o, s = divmod(i, NS)
                            dve.wait_ge(xp_pe.h, xp_pe.at(gb, 2 * (i + 1)))
                            ins = dve.tensor_copy(xdt[o][0:2 * XD, s * SL:(s + 1) * SL], bank(4 + i % 4, 2 * XD))
                            if mixed[li]:
                                if o == 1 and s == 0:
                                    dve.wait_ge(cv_act.h, cv_act.at(gb, 2 * NS))
                                ins = dve.tensor_copy(xdr[o][0:2 * XD, L - (s + 1) * SL:L - s * SL],
                                                      bank(4 + i % 4, 2 * XD)[:, ::-1])
                            ins.then_inc(xp_dve.h, 2)
                            if i == NS - 1:
                                dve.wait_ge(cv_act.h, cv_act.at(gb, 2 * NS))
                                dve.tensor_copy(wA.rearrange("p (a b) -> p a b", b=HH), by_columns(xcA)).then_inc(pm_dve.h, K)

                    dve.wait_ge(ca.h, ca.at(gb, 0))
                    dve.memset(carry[:], 0.0).then_inc(cz.h, 1)
                    dve.wait_ge(cz.h, cz.at(gb, 1))

                    def unit(c, k, t):
                        u = uno(c, k, t)
                        if t == 0:
                            loaded(dve, li, b, c, k)
                        dve.wait_ge(du_f.h, du_f.at(gb, u + 1))
                        dve.tensor_tensor(ps_du[t % 2], ps_du[t % 2], bt[k % 2], ALU.mult).then_inc(dbu.h, 1)
                        dve.wait_ge(ex.h, ex.at(gb, u + 1))
                        dve.wait_ge(yq.h, yq.at(gb, cno(c, k) * 6 + (t // 4 - 1)))
                        dve.wait_ge(dbu.h, dbu.at(gb, u + 1))
                        col = k * UN + t
                        way = slice(None, None, -1 if reverse(spec["dirs"][k]) else 1)
                        dve.tensor_tensor_scan(state[t % RH][:, way], decay[t % RDA][:, way], ps_du[t % 2][:, way], carry[:, col:col + 1],
                                               ALU.mult, ALU.add).then_inc(sc.h, 1)

                    def out_y(c, k, half):
                        n, m, kind = cno(c, k), (P, DB)[half], spec["dirs"][k]
                        dve.wait_ge(yq.h, yq.at(gb, n * 6 + (4 if half == 0 else 6)))
                        if tab:
                            st, o, vec = ((stA, yoA, vecA), (stB, yoB, vecB))[half]
                            dve.wait_ge(st.h, st.at(tb, n * 16))
                            dve.scalar_tensor_tensor(o[0:m, :], x_tiles(tab, k)[half][0:m, :], vec[:, V_D + k:V_D + k + 1],
                                                     ps_y[0:m, :], ALU.mult, ALU.add).then_inc(ev.h, 1)
                        else:
                            dve.wait_ge(ys0.h, ys0.at(nb, 2))
                            dve.wait_ge(ev.h, ev.at(gb, n * 2))
                            lines = span(place_of(c, kind), CH // WW)
                            image = y_sum[half][0:m, :].rearrange("p (h w) -> p h w" if stored(kind) == 0 else "p (h w) -> p w h", w=WW)
                            dve.tensor_tensor(image[:, lines, :], image[:, lines, :],
                                              ps_y[0:m, :].rearrange("p (a b) -> p a b", b=WW), ALU.add).then_inc(ev.h, 1)

                    def rest(c, k, half):
                        n, m = cno(c, k) * 2 + half, (P, DB)[half]
                        dve.wait_ge(sp_w.h, sp_w.at(gb, n + 1))
                        dve.scalar_tensor_tensor(az[half][0:m, :], wz[0:m, :], -1.0, az[half][0:m, :], ALU.add, ALU.subtract).then_inc(sp_r.h, 1)

                    def du_b(c, k):
                        dve.wait_ge(dt_ok.h, dt_ok.at(gb, cno(c, k) * 2 + 2))
                        loaded(dve, li, b, c, k)
                        dve.tensor_tensor(rz[1][DB:P, :], rz[1][0:DB, :], x_tiles(tab, k)[1][0:DB, :], ALU.mult).then_inc(du_ok.h, 1)

                    def norm_again(dst):
                        dve.wait_ge(x_again.h, x_again.at(gb, 16))
                        dve.wait_ge(du_f.h, du_f.at(gb, (CHK - 1) * UN))
                        dve.tensor_scalar(dst[0:DM, :], x_all[0:DM, :], gn_v[:, 4:5], gn_v[:, 7:8],
                                          ALU.subtract, ALU.mult).then_inc(xg_ok.h, 1)

                    def body(c, k, last):
                        for t in range(LEAD, UN if last else UN + LEAD):
                            if t < UN:
                                unit(c, k, t)
                            else:
                                unit(*nxt(c, k), t - UN)
                            if not last:
                                if t == REST_AT[0]:
                                    rest(*nxt(c, k), 0)
                                if t == REST_AT[1]:
                                    rest(*nxt(c, k), 1)
                            if t == DU_B_AT:
                                du_b(c, k)
                            if t == OUT_A_AT:
                                out_y(c, k, 0)
                            if last and t == 16 and not tab:
                                norm_again(xg)
                        out_y(c, k, 1)

                    rest(0, 0, 0)
                    rest(0, 0, 1)
                    for t in range(LEAD):
                        unit(0, 0, t)
                    chunks(dve, body)

                    if tab:
                        dve.wait_ge(yr_ld.h, yr_ld.at(tb, K * 16))
                        dve.tensor_tensor(ytok[0], ytok[0], ytok[1], ALU.add).then_inc(yr_ad.h, 1)
                        dve.tensor_tensor(ytok[2], ytok[2], ytok[3], ALU.add).then_inc(yr_ad.h, 1)
                        dve.wait_ge(yr_ad.h, yr_ad.at(tb, 2))
                        dve.tensor_tensor(ytok[0], ytok[0], ytok[2], ALU.add).then_inc(yr_ad.h, 1)
                        dve.wait_ge(yr_ad.h, yr_ad.at(tb, 3))
                        norm_again(xg_tab)
                        for i in range(2 * NS):
                            m, half = divmod(i, 2)
                            w = (P, DB)[half]
                            dve.wait_ge(yb_pe.h, yb_pe.at(tb, i + 1))
                            dve.tensor_copy(y_sum[half][0:w, m * SL:(m + 1) * SL], bank(i % 4, w)).then_inc(yb_cp.h, 1)
                    dve.wait_ge(ev.h, ev.at(gb, CHK * 2))
                    for s in range(NS + 4):
                        if s < NS:
                            dve.wait_ge(mu_pe.h, mu_pe.at(gb, s + 1))
                            cols = slice(s * SL, (s + 1) * SL)
                            for m, yy in ((P, y_sum[0]), (DB, y_sum[1])):
                                ins = dve.tensor_tensor(yy[0:m, cols], yy[0:m, cols], bank(6 + s % 2, m), ALU.subtract)
                            ins.then_inc(yc.h, 1)
                        v = s - 2
                        if 0 <= v < NS:
                            dve.wait_ge(rs_act.h, rs_act.at(gb, v + 1))
                            cols = slice(v * SL, (v + 1) * SL)
                            for m, yy in ((P, y_sum[0]), (DB, y_sum[1])):
                                ins = dve.tensor_tensor(yy[0:m, cols], yy[0:m, cols], rs[v % 3][0:m, :], ALU.mult)
                            ins.then_inc(yn.h, 1)
                        o = s - 4
                        if 0 <= o < NS:
                            dve.wait_ge(op_pe.h, op_pe.at(gb, o + 1))
                            dve.wait_ge(xo_st[o % 2].h, xo_st[o % 2].at(gb, o // 2 * 16))
                            dve.tensor_tensor(xout[o % 2][0:DM, :], x_all[0:DM, o * SL:(o + 1) * SL], bank(4 + o % 2, DM), ALU.add).then_inc(xo.h, 1)

        @block.gpsimd
        def _(pool):
            credit(pool, xz, pr, sp_s, dt_ok, du_ok, lo_ok, gt)
            pool.wait_ge(const_in, 96)
            for li, spec, g0, tab in per_layer():
                pool.wait_ge(wts_ok, ready[li])
                with pool.Fori(0, B) as b:
                    gb, tb, nb = (b, g0), (b, 0), (b, g0 - B * sum(is_tab[:li]))
                    pool.wait_ge(xo.h, xo.at(gb, 0))
                    passed(pool)
                    pool.memset(xn[0:DM, :], 0.0).then_inc(xz.h, 1)
                    if tab:
                        pool.wait_ge(tk_st.h, tk_st.at(tb, 64))
                        for k in range(K):
                            if k >= 2:
                                pool.wait_ge(gb_pe.h, gb_pe.at(tb, (k - 1) * NS))
                                pool.wait_ge(ga_pe.h, ga_pe.at(tb, (k - 1) * NS))
                            passed(pool)
                            for blk in range(BLK):
                                pool.indirect_dma_start(
                                    out=tok_g[k % 2][:, blk * DI:(blk + 1) * DI], out_offset=None, in_=xtok_d,
                                    in_offset=bass.IndirectOffsetOnAxis(ap=order[:, k * BLK + blk:k * BLK + blk + 1], axis=0),
                                ).then_inc(tg[k % 2].h, 16)

                    def unit(c, k, t):
                        pool.wait_ge(ca.h, ca.at(gb, uno(c, k, t) + 1))
                        pool.tensor_tensor(state[t % RH], state[t % RH], ct[k % 2], ALU.mult).then_inc(pr.h, 1)

                    def soft(c, k, half, step):
                        m, n = (P, DB)[half], cno(c, k) * 2 + half
                        if step == 0:
                            pool.wait_ge(sp_r.h, sp_r.at(gb, n + 1))
                            pool.tensor_tensor(rz[half][0:m, :], rz[half][0:m, :], az[half][0:m, :], ALU.subtract).then_inc(sp_s.h, 1)
                        elif step == 1:
                            pool.wait_ge(sp_l.h, sp_l.at(gb, n + 1))
                            pool.wait_ge(sp_s.h, sp_s.at(gb, n + 1))
                            pool.tensor_tensor(rz[half][0:m, :], rz[half][0:m, :], lz[0:m, :], ALU.add).then_inc(dt_ok.h, 1)
                        else:
                            pool.wait_ge(dt_ok.h, dt_ok.at(gb, n + 1))
                            loaded(pool, li, b, c, k)
                            pool.tensor_tensor(az[half][0:m, :], rz[half][0:m, :], x_tiles(tab, k)[0], ALU.mult).then_inc(du_ok.h, 1)

                    def split(c, k, i):
                        tile = ("dtA", "duA", "mixB")[i]
                        pool.wait_ge(hi_ok.h, hi_ok.at(gb, cno(c, k) * 3 + i + 1))
                        pool.tensor_tensor(lo[tile][k % 2], (rz[0], az[0], rz[1])[i], hi[tile][k % 2].bitcast(F32),
                                           ALU.subtract).then_inc(lo_ok.h, 1)

                    def body(c, k, last):
                        for t in range(LEAD, UN if last else UN + LEAD):
                            if t < UN:
                                unit(c, k, t)
                            else:
                                unit(*nxt(c, k), t - UN)
                            for what, *args in POOL_STEPS.get(t, ()):
                                if args == [2]:
                                    split(c, k, 2)
                                elif not last:
                                    (soft if what == "soft" else split)(*nxt(c, k), *args)

                    for fn, *args in ((soft, 0, 0), (soft, 0, 1), (soft, 0, 2), (split, 0), (split, 1),
                                      (soft, 1, 0), (soft, 1, 1)):
                        fn(0, 0, *args)
                    for t in range(LEAD):
                        unit(0, 0, t)
                    chunks(pool, body)

                    if tab:
                        for k in range(K):
                            for blk in range(BLK):
                                if blk % 4 == 0:
                                    pool.wait_ge(yt_act.h, yt_act.at(tb, k * BLK // 2 + blk // 2 + 2))
                                    passed(pool)
                                pool.indirect_dma_start(
                                    out=ytok_d[k], out_offset=bass.IndirectOffsetOnAxis(
                                        ap=order[:, k * BLK + blk:k * BLK + blk + 1], axis=0),
                                    in_=tok_o[k % 2][:, blk * DI:(blk + 1) * DI], in_offset=None,
                                ).then_inc(ys_st[k].h, 16)
                    for s in range(NS):
                        pool.wait_ge(af.h, af.at(gb, s + 1))
                        pool.wait_ge(zz_act.h, zz_act.at(gb, 2 * NS))
                        cols = slice(s * SL, (s + 1) * SL)
                        for m, yy, zz in zip((P, DB), y_sum, gates_tab if tab else gates):
                            ins = pool.tensor_tensor(yy[0:m, cols], yy[0:m, cols], zz[0:m, cols], ALU.mult)
                        ins.then_inc(gt.h, 1)


def scan_orders():
    o1, o2 = [], []
    for s in range(HH + WW - 1):
        ii = range(max(0, s - WW + 1), min(HH, s + 1))
        for o, coords in ((o1, [i * WW + (s - i) for i in ii]),
                          (o2, [i * WW + WW - 1 - (s - i) for i in ii if 0 <= WW - 1 - (s - i) < WW])):
            o.extend(coords[::-1] if s % 2 == 1 else coords)
    yy, xx = np.meshgrid(np.arange(HH), np.arange(WW), indexing="ij")
    dy, dx = yy - HH // 2, xx - WW // 2
    r = np.sqrt(dy ** 2 + dx ** 2)
    th = np.arctan2(dy, dx)
    o3 = np.argsort((r * (L + 1) + (th + np.pi) * 10).flatten())
    o4 = np.argsort((-r * (L + 1) + (th + np.pi) * 10).flatten())
    return np.stack([np.array(o1), np.array(o2), o3, o4])


def constants():
    f = np.float32
    p = np.arange(P)
    spread = np.zeros((P, 4, 4, P), f)
    gather = np.zeros((P, 4, 32), f)
    for q in range(4):
        for d in range(G8):
            for r in range(4):
                spread[32 * r + 8 * q + d, r, q, d::G8] = 1
            gather[np.ix_(p[p % G8 == d], [q], [8 * q + d])] = 1
    c = np.arange(DM)
    mean3 = (c[:, None] // 3 == c[None, :] // 3).astype(f) / f(3)
    idx = scan_orders()
    i = np.arange(HH, dtype=f)
    yy, xx = np.meshgrid((i - f(HH / 2)) / f(HH / 2), (i - f(WW / 2)) / f(WW / 2), indexing="ij")
    r = np.minimum(np.sqrt(yy ** 2 + xx ** 2), f(2.0))
    th = np.arctan2(yy, xx) / f(np.pi)
    coords = np.stack([r.ravel(), th.ravel()]).astype(f)[:, idx.ravel()]
    return {
        "c_ident": np.eye(P, dtype=f), "c_spread": spread.reshape(P, -1), "c_gather8": gather.reshape(P, -1),
        "c_mean192": np.full((P, P), 1 / DI, f), "c_mean3": mean3, "c_coords": coords,
        "c_order": np.ascontiguousarray(idx.reshape(K * BLK, P).T).astype(np.uint32),
    }


def laid_out(name, a):
    a = np.asarray(a)
    tail = name.split("conv_", 1)[-1]
    if name == "x":
        a = a.reshape(a.shape[0], L, DM).transpose(0, 2, 1)
    elif tail in ("in_proj_w", "out_proj_w", "direction_Bs", "pf_w1", "pf_w2"):
        a = a.T
    elif tail == "conv_w":
        a = a.reshape(DI, 9).T.reshape(9 * DI)
    elif tail in ("x_proj_w", "x_proj_weight"):
        a = a.reshape(K * XD, DI).T
    elif tail in ("dt_projs_w", "dt_projs_weight"):
        a = a.reshape(K * DI, R).T
    elif tail == "A_logs":
        a = a.reshape(K, DI, N)
        first = a[:, :P].reshape(K, 4, 4, G8, N).transpose(4, 3, 0, 2, 1).reshape(P, K, UA)
        second = a[:, P:].reshape(K, 2, 4, G8, N).transpose(4, 3, 0, 2, 1).reshape(P, K, UN - UA)
        a = np.concatenate([first, second], axis=2).reshape(P, K * UN)
    elif tail in ("Ds", "dt_projs_bias"):
        a = a.reshape(K, DI).T
    elif tail == "pf_b2":
        a = a.reshape(K)
    else:
        a = a.reshape(-1, 1)
    return np.ascontiguousarray(a)


def kernel(**inputs):
    import concourse.bacc as bacc
    from concourse.bass_utils import run_bass_kernel_spmd

    nc = bacc.Bacc("TRN2", target_bir_lowering=False, num_devices=1)
    arrays, t_in = {}, {}
    for name, a in {**{n: laid_out(n, v) for n, v in inputs.items()}, **constants()}.items():
        arrays["in_" + name] = a
        t_in[name] = nc.dram_tensor("in_" + name, a.shape, mybir.dt.from_np(a.dtype), kind="ExternalInput").ap()
    B = arrays["in_x"].shape[0]
    out = nc.dram_tensor("out_x", [B, DM, L], F32, kind="ExternalOutput").ap()
    build(nc, B, LAYERS, t_in, out)
    r = run_bass_kernel_spmd(nc, [arrays], core_ids=[0])
    return np.ascontiguousarray(r.results[0]["out_x"].transpose(0, 2, 1)).reshape(B, HH, WW, DM)
```
